# Optimizing a Trainium2 kernel written in Bass

```python
import numpy as np
import jax
import jax.numpy as jnp

def _softmax(x, axis=-1):
    return jax.nn.softmax(x, axis=axis)

def _gelu(x):
    return jax.nn.gelu(x, approximate=True)

def _silu(x):
    return jax.nn.silu(x)

def _sigmoid(x):
    return jax.nn.sigmoid(x)

def _layernorm(x, axis=-1, eps=1e-05):
    m = jnp.mean(x, axis=axis, keepdims=True)
    v = jnp.var(x, axis=axis, keepdims=True)
    return (x - m) / jnp.sqrt(v + eps)

def _scatter_add(tgt, idx, src, axis=0):
    return tgt.at[idx].add(src)

def _segment_sum(src, seg, n):
    return jax.ops.segment_sum(src, seg, n)
kernel_name = 'mk_adj_preln_d1_adj_r2_0ad647'

def setup_inputs(seed: int=0):
    np.random.seed(seed)
    _w = jnp.asarray

    def _rec_inputs():
        import jax
        import jax.numpy as jnp
        _gk = jax.random.key(seed)
        x = 7.22e-05 + 1 * jax.random.normal(jax.random.fold_in(_gk, 1), (64, 128, 1024), jnp.float32)
        _a = jax.random.bernoulli(jax.random.fold_in(_gk, 2), 0.0625, (128, 128))
        _a = jnp.logical_or(_a, jnp.swapaxes(_a, -1, -2))
        _a = jnp.logical_or(_a, jnp.eye(128, dtype=bool))
        _af = _a.astype(jnp.float32)
        _af = _af * jax.random.uniform(jax.random.fold_in(_gk, 3), (128, 128), jnp.float32, 0.05, 0.27663)
        adj = _af
        return (x, adj)
    x, adj = _rec_inputs()

    def _L0_gnn_setup():
        import jax, jax.numpy as jnp
        import numpy as np
        N, B, T = (1024, 16, 128)
        key = jax.random.key(seed)
        k1, k2, k3, k4 = jax.random.split(key, 4)
        x = jax.random.normal(k1, (B, T, N), dtype=jnp.float32)
        weight = jax.random.normal(k2, (T, T), dtype=jnp.float32) * (1.0 / np.sqrt(T))
        bias = jax.random.normal(k3, (T,), dtype=jnp.float32) * 0.01
        u = jax.random.uniform(k4, (N * N, 2), dtype=jnp.float32, minval=1e-06, maxval=1.0 - 1e-06)
        gumbel = -jnp.log(-jnp.log(u))
        return {'x': x, 'weight': weight, 'bias': bias, 'gumbel': gumbel}
    _L0_gnn_all = _L0_gnn_setup()
    _L0_gnn_in = {k: v for k, v in _L0_gnn_all.items() if k in ('bias', 'gumbel')}
    del _L0_gnn_all
    return {'x': x, 'adj': adj, 'L0_gnn_bias': _L0_gnn_in['bias'], 'L0_gnn_gumbel': _L0_gnn_in['gumbel']}

def reference(x, adj, L0_gnn_bias, L0_gnn_gumbel):
    import jax
    import jax.numpy as jnp

    def _L0_gnn_ref(x, weight, bias, gumbel):
        import jax, jax.numpy as jnp
        import numpy as np
        N, B, T = (1024, 16, 128)
        xp = jnp.transpose(x, (2, 0, 1))
        n = xp.shape[0]
        xs = jax.lax.stop_gradient(xp)
        x_avg = xs.mean(axis=1)
        x_norm = x_avg / jnp.maximum(jnp.linalg.norm(x_avg, axis=-1, keepdims=True), 1e-12)
        sim = (x_norm @ x_norm.T + 1.0) * 0.5
        sim_flat = sim.reshape(-1)
        score0 = sim_flat + gumbel[:, 0]
        score1 = 1.0 - sim_flat + gumbel[:, 1]
        adj = (score0 > score1).astype(xp.dtype).reshape(n, n)
        adj_sym = jnp.clip(adj + adj.T, 0.0, 1.0)
        nmask = jnp.clip(adj_sym + jnp.eye(n, dtype=xp.dtype), 0.0, 1.0)
        common = nmask @ nmask.T
        max_common = common.max()
        valid = adj_sym * (common > 1.0).astype(xp.dtype) > 0
        struct = jnp.where(valid, common / max_common * common, 0.0)
        W = adj * struct
        deg = W.sum(axis=0)
        dinv = jnp.where(deg > 0, deg ** (-0.5), 0.0)
        Wn = dinv[:, None] * W * dinv[None, :]
        xw = jnp.einsum('nbt,to->nbo', xp, weight)
        out = jnp.einsum('sd,sbt->dbt', Wn, xw) + bias
        return jnp.transpose(out, (1, 2, 0))
    h = jnp.maximum(_layernorm(x, axis=-1), 0.0)
    x = x + _L0_gnn_ref(h, adj, L0_gnn_bias, L0_gnn_gumbel)
    return x

_drawn_inputs = setup_inputs


def setup_inputs(seed=0):
    import zlib

    import numpy as np

    out = dict(_drawn_inputs(seed))
    spreads = {}
    factors = {'L0_gnn_bias': 8.0, 'L0_gnn_gumbel': 12.466}
    for name, (base, spread) in spreads.items():
        noise = np.random.default_rng([zlib.crc32(name.encode()), seed]).standard_normal(out[name].shape)
        drawn = base * np.exp(spread * noise) if base else spread * noise
        out[name] = jnp.asarray(drawn.astype(out[name].dtype))
    for name, factor in factors.items():
        out[name] = (out[name] * factor).astype(out[name].dtype)
    return out
```

```python
from contextlib import ExitStack

import concourse.bass as bass
from concourse import mybir

FP32 = mybir.dt.float32
BF16 = mybir.dt.bfloat16
ALU = mybir.AluOpType
ACT = mybir.ActivationFunctionType
AX_X = mybir.AxisListType.X
RMAX = bass.bass_isa.ReduceOp.max


def gnn_kernel(nc, x, weight, bias, gumbel, out):
    B, T, N = x.shape
    C = N // 128
    HALF = 512
    PAIRS = B // 2
    EPS = 1e-5
    GROUP = 8
    ROUNDS = B // GROUP
    KEPT = 2 * ROUNDS
    XPAIRS = 8
    XSLOTS = 4

    gum = gumbel.rearrange("(c p d) k -> c p (d k)", c=C, p=128)
    bias_col = bias.rearrange("(p a) -> p a", a=1)

    ctx = ExitStack()
    with ctx:
        def sb(name, shape, dt=FP32):
            return ctx.enter_context(nc.sbuf_tensor(name, shape, dt))

        def sem(name):
            return ctx.enter_context(nc.semaphore(name))

        ident = sb("ident", [128, 128])
        identb = sb("identb", [128, 128], BF16)
        ones = sb("ones", [128, 128])
        w_sb = sb("w_sb", [128, T])
        bias_sb = sb("bias_sb", [128, 1])
        eps_sb = sb("eps_sb", [128, 1])
        rstd = sb("rstd", [128, B])
        shift = sb("shift", [128, B])
        stats = sb("stats", [128, 2, 2, 12])
        mv = sb("mv", [128, 2, 2, 2])
        small = sb("small", [128, 2, 6, 2])
        node = sb("node", [128, 10, C])
        dmax = sb("dmax", [128, 4])
        hsum = sb("hsum", [128, N])
        wide = sb("wide", [128, N])
        kept = sb("kept", [128, KEPT, N])

        region1 = sb("region1", [128, XPAIRS * 2 * N])
        xin = region1[:, :].rearrange("p (s b n) -> p s b n", s=XPAIRS, b=2)
        graph = region1[:, 0:C * N].rearrange("p (c n) -> p c n", c=C)
        squares = region1[:, C * N:(C + 2) * N].rearrange("p (s n) -> p s n", s=2)
        masks = region1[:, (C + 2) * N:(C + 3) * N].bitcast(BF16).rearrange("p (s n) -> p s n", s=2)
        region2 = sb("region2", [128, 16 * N])
        h1 = region2[:, 0:4 * N].rearrange("p (s n) -> p s n", s=4)
        sim = region2[:, 0:2 * N].rearrange("p (s n) -> p s n", s=2)
        dis = region2[:, 2 * N:4 * N].rearrange("p (s n) -> p s n", s=2)
        gin = region2[:, 4 * N:8 * N].rearrange("p (s n k) -> p s n k", s=2, k=2)
        adj = region2[:, 8 * N:12 * N].bitcast(BF16).rearrange("p (c n) -> p c n", c=C)
        nmask = region2[:, 12 * N:16 * N].bitcast(BF16).rearrange("p (c n) -> p c n", c=C)
        x2 = region2[:, 0:4 * N].rearrange("p (s n) -> p s n", s=4)
        h2 = region2[:, 4 * N:6 * N].rearrange("p (s n) -> p s n", s=2)
        xw = region2[:, 6 * N:8 * N].rearrange("p (s c o) -> p s c o", s=2, c=C)

        ps = ctx.enter_context(nc.psum_tensor("ps", [128, 8, HALF], FP32))

        def bank(k, n=1):
            return ps[:, k:k + n, :].rearrange("p k n -> p (k n)")

        s_const = sem("s_const")
        s_in = sem("s_in")
        s_x = [sem(f"s_x{k}") for k in range(XPAIRS)]
        s_bn = sem("s_bn")
        s_mv = sem("s_mv")
        s_std = sem("s_std")
        s_newton = sem("s_newton")
        s_row = sem("s_row")
        s_h = sem("s_h")
        s_even = sem("s_even")
        s_odd = sem("s_odd")
        s_hw = sem("s_hw")
        s_kept = sem("s_kept")
        s_dve = sem("s_dve")
        s_sum = sem("s_sum")
        s_sq = sem("s_sq")
        s_col = sem("s_col")
        s_guard = sem("s_guard")
        s_root = sem("s_root")
        s_diag = sem("s_diag")
        s_rep = sem("s_rep")
        s_unit = sem("s_unit")
        s_g = [sem(f"s_g{k}") for k in range(2)]
        s_dot = sem("s_dot")
        s_sim = sem("s_sim")
        s_dis = sem("s_dis")
        s_score0 = sem("s_score0")
        s_score1 = sem("s_score1")
        s_adj = sem("s_adj")
        s_tr = sem("s_tr")
        s_sym = sem("s_sym")
        s_nm = sem("s_nm")
        s_cnt = sem("s_cnt")
        s_pmax = sem("s_pmax")
        s_gmax = sem("s_gmax")
        s_com = sem("s_com")
        s_csq = sem("s_csq")
        s_mask = sem("s_mask")
        s_edge = sem("s_edge")
        s_colsum = sem("s_colsum")
        s_wn = sem("s_wn")
        s_x2 = [sem(f"s_x2{k}") for k in range(XSLOTS)]
        s_h2 = sem("s_h2")
        s_hw2 = sem("s_hw2")
        s_xw = sem("s_xw")
        s_mm = sem("s_mm")
        s_res = sem("s_res")
        s_st = [sem(f"s_st{k}") for k in range(XSLOTS)]
        block = ctx.enter_context(nc.Block())

        def wait(eng, s, value):
            if not isinstance(value, int) or value > 0:
                eng.wait_ge(s, value)

        def rounds(eng, count, body):
            body(0)
            with eng.Fori(1, count) as r:
                body(r)

        def blk(j):
            return slice(128 * j, 128 * j + 128)

        def half(j):
            return slice(HALF * j, HALF * j + HALF)

        PSUM3 = (0, 2, 6)

        @block.sync
        def _(sp):
            sp.dma_start(w_sb[:, :], weight).then_inc(s_in, 16)
            sp.dma_start(bias_sb[:, :], bias_col).then_inc(s_in, 16)

            def load_pairs(r):
                for k in range(XPAIRS):
                    wait(sp, s_h, (r - 1) * (2 * XPAIRS) + 2 * k + 2)
                    sp.dma_start(xin[:, k, :, :],
                                 x[bass.ds(r * (2 * XPAIRS) + 2 * k, 2), :, :].rearrange("b t n -> t b n")
                                 ).then_inc(s_x[k], 16)

            rounds(sp, PAIRS // XPAIRS, load_pairs)
            for i in range(C):
                if i >= 2:
                    sp.wait_ge(s_adj, i - 1)
                sp.dma_start(gin[:, i % 2, :, :].rearrange("p n k -> p (n k)"), gum[i, :, :]).then_inc(s_g[i % 2], 16)
            sp.wait_ge(s_adj, C)

            def load_batches(q):
                for j in range(GROUP):
                    slot = j % XSLOTS
                    wait(sp, s_st[slot], 16 * (q * (GROUP // XSLOTS) + j // XSLOTS))
                    sp.dma_start(x2[:, slot, :], x[q * GROUP + j, :, :]).then_inc(s_x2[slot], 16)

            rounds(sp, ROUNDS, load_batches)

        @block.gpsimd
        def _(pool):
            pool.memset(ones[:, :], 1.0).then_inc(s_const, 1)
            pool.memset(eps_sb[:, :], EPS).then_inc(s_const, 1)
            pool.memset(hsum[:, :], 0.0).then_inc(s_const, 1)
            pool.wait_ge(s_const, 3)
            pool.affine_select(out=ident[:, :], in_=ones[:, :], compare_op=ALU.is_equal, fill=0.0, base=0,
                               pattern=[[-1, 128]], channel_multiplier=1).then_inc(s_const, 1)
            pool.wait_ge(s_const, 4)
            pool.tensor_copy(identb[:, :], ident[:, :]).then_inc(s_const, 1)

            def add_even(r):
                for k in range(XPAIRS):
                    pair = r * XPAIRS + k
                    pool.wait_ge(s_h, pair * 2 + 1)
                    wait(pool, s_even, pair)
                    pool.tensor_tensor(hsum[:, :], hsum[:, :], h1[:, 2 * (k % 2), :], ALU.add).then_inc(s_even, 1)

            rounds(pool, PAIRS // XPAIRS, add_even)

            for i in range(C):
                pool.wait_ge(s_dis, i + 1)
                pool.wait_ge(s_g[i % 2], 16 * (i // 2 + 1))
                pool.tensor_tensor(dis[:, i % 2, :], dis[:, i % 2, :], gin[:, i % 2, :, 1], ALU.add
                                   ).then_inc(s_score1, 1)
            pool.wait_ge(s_pmax, 1)
            pool.partition_all_reduce(dmax[:, 1:2], dmax[:, 0:1], 128, RMAX).then_inc(s_gmax, 1)
            for i in range(1, C):
                pool.wait_ge(s_edge, i + 1)
                if i > 1:
                    pool.wait_ge(s_colsum, i - 1)
                pool.tensor_tensor(wide[:, :], graph[:, 0, :] if i == 1 else wide[:, :], graph[:, i, :], ALU.add
                                   ).then_inc(s_colsum, 1)

            def store_batches(q):
                for j in range(GROUP):
                    pool.wait_ge(s_res, q * GROUP + j + 1)
                    pool.dma_start(out[q * GROUP + j, :, :], x2[:, j % XSLOTS, :]).then_inc(s_st[j % XSLOTS], 16)

            rounds(pool, ROUNDS, store_batches)
            for slot in range(XSLOTS):
                pool.wait_ge(s_st[slot], 16 * (B // XSLOTS))

        @block.scalar
        def _(act):
            act.wait_ge(s_const, 2)

            def std(k, pair):
                act.wait_ge(s_mv, pair + 1)
                act.activation(small[:, k % 2, 0, :], mv[:, k % 2, :, 1], ACT.Sqrt, bias=eps_sb[:, :]
                               ).then_inc(s_std, 1)

            def relu(k, pair):
                act.wait_ge(s_row, pair + 1)
                wait(act, s_even, pair - 1)
                wait(act, s_odd, pair - 1)
                for b in range(2):
                    n = pair * 2 + b
                    act.activation(h1[:, 2 * (k % 2) + b, :], xin[:, k % XPAIRS, b, :], ACT.Relu,
                                   bias=shift[:, bass.ds(n, 1)], scale=rstd[:, bass.ds(n, 1)]).then_inc(s_h, 1)

            def first(r):
                for k in range(XPAIRS):
                    pair = r * XPAIRS + k
                    std(k, pair)
                    if k or not isinstance(r, int):
                        relu((k - 1) % XPAIRS, pair - 1)
                    if k % 4 == 2:
                        for b in range(2):
                            n = r * 4 + k // 4 * 2 + b
                            act.wait_ge(s_hw, n + 1)
                            act.activation(kept[:, bass.ds(n, 1), :], bank(2 + 2 * b, 2).rearrange("p (a n) -> p a n", a=1),
                                           ACT.Copy).then_inc(s_kept, 1)

            rounds(act, PAIRS // XPAIRS, first)
            relu(XPAIRS - 1, PAIRS - 1)

            act.wait_ge(s_sum, 1)
            act.activation(wide[:, :], hsum[:, :], ACT.Square, scale=1.0 / B).then_inc(s_sq, 1)
            act.wait_ge(s_guard, 1)
            act.activation(node[:, 1, :], node[:, 0, :], ACT.Sqrt).then_inc(s_root, 1)
            for i in range(C):
                act.wait_ge(s_dot, i + 1)
                if i >= 2:
                    act.wait_ge(s_adj, i - 1)
                act.activation(sim[:, i % 2, :], bank(PSUM3[i % 3], 2), ACT.Copy, scale=0.5, bias=0.5
                               ).then_inc(s_sim, 1)
                act.wait_ge(s_sim, i + 1)
                act.activation(dis[:, i % 2, :], sim[:, i % 2, :], ACT.Copy, scale=-1.0, bias=1.0).then_inc(s_dis, 1)
            for i in range(C):
                act.wait_ge(s_nm, i + 1)
                if i >= 2:
                    act.wait_ge(s_cnt, i - 1)
                act.activation(squares[:, i % 2, :], nmask[:, i, :], ACT.Copy, accum_out=node[:, 6, i:i + 1]
                               ).then_inc(s_cnt, 1)
            act.wait_ge(s_cnt, C)
            for i in range(C):
                act.wait_ge(s_com, i + 1)
                if i >= 2:
                    act.wait_ge(s_edge, i - 1)
                act.activation(squares[:, i % 2, :], bank(PSUM3[i % 3], 2), ACT.Square).then_inc(s_csq, 1)
            act.wait_ge(s_guard, 2)
            act.activation(node[:, 1, :], node[:, 0, :], ACT.Sqrt).then_inc(s_root, 1)

            def second(q):
                for j in range(GROUP):
                    n = q * GROUP + j
                    if 1 <= j < GROUP - 1:
                        m = q * (GROUP - 2) + j - 1
                        act.wait_ge(s_x2[(j + 1) % XSLOTS], 16 * (q * (GROUP // XSLOTS) + (j + 1) // XSLOTS + 1))
                        wait(act, s_hw2, m - 1)
                        act.activation(h2[:, (j + 1) % 2, :], x2[:, (j + 1) % XSLOTS, :], ACT.Relu,
                                       bias=shift[:, bass.ds(n + 1, 1)], scale=rstd[:, bass.ds(n + 1, 1)]
                                       ).then_inc(s_h2, 1)
                    wait(act, s_mm, n - 1)
                    to = xw[:, j % 2, :, :].rearrange("p c o -> p (c o)")
                    if j < 2:
                        act.activation(to.rearrange("p (a n) -> p a n", a=1), kept[:, bass.ds(q * 2 + j, 1), :],
                                       ACT.Copy).then_inc(s_xw, 1)
                    else:
                        act.wait_ge(s_hw2, q * (GROUP - 2) + j - 1)
                        act.activation(to, bank(4, 2), ACT.Copy).then_inc(s_xw, 1)

            rounds(act, ROUNDS, second)

        @block.vector
        def _(dve):
            dve.wait_ge(s_const, 5)
            dve.wait_ge(s_in, 32)

            def bn(k, r, pair):
                dve.wait_ge(s_x[k], (r + 1) * 16)
                for b in range(2):
                    for f in range(2):
                        last = dve.bn_stats(stats[:, k % 2, b, 6 * f:6 * f + 6], xin[:, k, b, half(f)])
                last.then_inc(s_bn, 1)
                dve.wait_ge(s_bn, pair + 1)

            def aggregate(k):
                for b in range(2):
                    last = dve.bn_aggr(mv[:, k % 2, b, :], stats[:, k % 2, b, :])
                last.then_inc(s_mv, 1)

            def row(k, pair):
                root, inv, t1, t2, t3 = (small[:, k % 2, c, :] for c in range(5))
                mean, var = mv[:, k % 2, :, 0], mv[:, k % 2, :, 1]
                here = bass.ds(pair * 2, 2)
                dve.wait_ge(s_std, pair + 1)
                dve.reciprocal(inv, root).then_inc(s_newton, 1)
                dve.wait_ge(s_newton, pair * 5 + 1)
                dve.tensor_tensor(t1, inv, inv, ALU.mult).then_inc(s_newton, 1)
                dve.wait_ge(s_newton, pair * 5 + 2)
                dve.scalar_tensor_tensor(out=t2, in0=var, scalar=EPS, in1=t1, op0=ALU.add, op1=ALU.mult
                                         ).then_inc(s_newton, 1)
                dve.wait_ge(s_newton, pair * 5 + 3)
                dve.tensor_scalar(t3, t2, -0.5, 1.5, ALU.mult, ALU.add).then_inc(s_newton, 1)
                dve.wait_ge(s_newton, pair * 5 + 4)
                dve.tensor_tensor(rstd[:, here], t3, inv, ALU.mult).then_inc(s_newton, 1)
                dve.wait_ge(s_newton, pair * 5 + 5)
                dve.scalar_tensor_tensor(out=shift[:, here], in0=mean, scalar=-1.0, in1=rstd[:, here],
                                         op0=ALU.mult, op1=ALU.mult).then_inc(s_row, 1)

            def first(r):
                for k in range(XPAIRS):
                    pair = r * XPAIRS + k
                    bn(k, r, pair)
                    if k or not isinstance(r, int):
                        row((k - 1) % XPAIRS, pair - 1)
                    aggregate(k)

            rounds(dve, PAIRS // XPAIRS, first)
            row(XPAIRS - 1, PAIRS - 1)

            chain = [0]

            def step(ins):
                chain[0] += 1
                ins.then_inc(s_dve, 1)
                dve.wait_ge(s_dve, chain[0])

            def inverse_root(n, scale):
                dve.wait_ge(s_root, n)
                step(dve.reciprocal(node[:, 2, :], node[:, 1, :]))
                step(dve.tensor_tensor(node[:, 3, :], node[:, 2, :], node[:, 2, :], ALU.mult))
                step(dve.tensor_tensor(node[:, 4, :], node[:, 3, :], node[:, 0, :], ALU.mult))
                step(dve.tensor_scalar(node[:, 3, :], node[:, 4, :], -0.5, 1.5, ALU.mult, ALU.add))
                step(dve.scalar_tensor_tensor(out=node[:, 5, :], in0=node[:, 3, :], scalar=scale, in1=node[:, 2, :],
                                              op0=ALU.mult, op1=ALU.mult))

            def diagonal():
                for j in range(C):
                    last = dve.tensor_scalar(wide[:, blk(j)], ident[:, :], node[:, 5, j:j + 1], None, ALU.mult)
                last.then_inc(s_diag, 1)

            dve.wait_ge(s_odd, PAIRS)
            dve.wait_ge(s_even, PAIRS)
            dve.tensor_tensor(hsum[:, :], bank(0, 2), hsum[:, :], ALU.add).then_inc(s_sum, 1)
            dve.wait_ge(s_col, 1)
            dve.tensor_scalar(node[:, 0, :], ps[:, 2, 0:C], 1e-24, None, ALU.max).then_inc(s_guard, 1)
            inverse_root(1, 1.0 / B)
            diagonal()
            dve.wait_ge(s_rep, 1)
            dve.tensor_tensor(hsum[:, :], bank(4, 2), hsum[:, :], ALU.mult).then_inc(s_unit, 1)

            def score0(i):
                dve.wait_ge(s_dis, i + 1)
                dve.wait_ge(s_g[i % 2], 16 * (i // 2 + 1))
                dve.tensor_tensor(sim[:, i % 2, :], sim[:, i % 2, :], gin[:, i % 2, :, 0], ALU.add
                                  ).then_inc(s_score0, 1)

            score0(0)
            for i in range(C):
                if i + 1 < C:
                    score0(i + 1)
                dve.wait_ge(s_score0, i + 1)
                dve.wait_ge(s_score1, i + 1)
                dve.tensor_tensor(adj[:, i, :], sim[:, i % 2, :], dis[:, i % 2, :], ALU.is_gt).then_inc(s_adj, 1)
            for i in range(C):
                dve.wait_ge(s_tr, i + 1)
                dve.tensor_tensor(nmask[:, i, :], ps[:, 4 + i % 2, :].bitcast(BF16), adj[:, i, :], ALU.max
                                  ).then_inc(s_sym, 1)
                dve.wait_ge(s_sym, i + 1)
                dve.tensor_tensor(nmask[:, i, blk(i)], nmask[:, i, blk(i)], identb[:, :], ALU.max).then_inc(s_nm, 1)
            dve.wait_ge(s_cnt, C)
            dve.reduce_max(dmax[:, 0:1], node[:, 6, :], AX_X).then_inc(s_pmax, 1)

            def mask(i):
                dve.wait_ge(s_csq, i + 1)
                dve.scalar_tensor_tensor(out=masks[:, i % 2, 0:N], in0=squares[:, i % 2, :], scalar=1.0,
                                         in1=adj[:, i, :], op0=ALU.is_gt, op1=ALU.mult).then_inc(s_mask, 1)

            mask(0)
            for i in range(C):
                if i + 1 < C:
                    mask(i + 1)
                dve.wait_ge(s_mask, i + 1)
                dve.tensor_tensor(graph[:, i, :], squares[:, i % 2, :], masks[:, i % 2, 0:N], ALU.mult
                                  ).then_inc(s_edge, 1)

            dve.wait_ge(s_gmax, 1)
            step(dve.reciprocal(dmax[:, 2:3], dmax[:, 1:2]))
            dve.wait_ge(s_col, 2)
            step(dve.tensor_scalar(node[:, 7, :], ps[:, 4, 0:C], dmax[:, 2:3], None, ALU.mult))
            dve.tensor_scalar(node[:, 0, :], node[:, 7, :], 1e-6, None, ALU.max).then_inc(s_guard, 1)
            step(dve.tensor_scalar(node[:, 8, :], node[:, 7, :], 0.0, None, ALU.is_gt))
            inverse_root(2, 1.0)
            step(dve.tensor_tensor(node[:, 5, :], node[:, 5, :], node[:, 8, :], ALU.mult))
            dve.tensor_scalar(node[:, 9, :], node[:, 5, :], dmax[:, 2:3], None, ALU.mult)
            diagonal()
            dve.wait_ge(s_diag, 2)
            dve.wait_ge(s_rep, 2)
            for i in range(C):
                dve.scalar_tensor_tensor(out=graph[:, i, :], in0=graph[:, i, :], scalar=node[:, 9, i:i + 1],
                                         in1=bank(6, 2), op0=ALU.mult, op1=ALU.mult).then_inc(s_wn, 1)

            def second(q):
                for j in range(GROUP):
                    n = q * GROUP + j
                    slot = j % XSLOTS
                    dve.wait_ge(s_x2[slot], 16 * (q * (GROUP // XSLOTS) + j // XSLOTS + 1))
                    dve.wait_ge(s_mm, n + 1)
                    for f in range(2):
                        last = dve.scalar_tensor_tensor(out=x2[:, slot, half(f)], in0=ps[:, 2 * (j % 2) + f, :],
                                                        scalar=bias_sb[:, :], in1=x2[:, slot, half(f)],
                                                        op0=ALU.add, op1=ALU.add)
                    last.then_inc(s_res, 1)

            rounds(dve, ROUNDS, second)

        @block.tensor
        def _(pe):
            pe.wait_ge(s_const, 5)
            pe.wait_ge(s_in, 32)

            def times_weight(h, first_bank):
                for c in range(C):
                    last = pe.matmul(ps[:, first_bank + c // 4, blk(c % 4)], h[:, blk(c)], w_sb[:, :],
                                     start=True, stop=True)
                return last

            def first(r):
                for k in range(XPAIRS):
                    pair = r * XPAIRS + k
                    if k % 4 == 0:
                        for b in range(2):
                            n = r * 4 + k // 4 * 2 + b
                            pe.wait_ge(s_h, pair * 2 + b + 1)
                            wait(pe, s_kept, n - 1)
                            times_weight(h1[:, 2 * (k % 2) + b, :], 2 + 2 * b).then_inc(s_hw, 1)
                    pe.wait_ge(s_h, pair * 2 + 2)
                    for f in range(2):
                        last = pe.matmul(ps[:, f, :], ident[:, :], h1[:, 2 * (k % 2) + 1, half(f)],
                                         start=isinstance(r, int) and k == 0, stop=True, skip_group_check=True)
                    last.then_inc(s_odd, 1)

            rounds(pe, PAIRS // XPAIRS, first)

            def column_sums(b):
                for j in range(C):
                    last = pe.matmul(ps[:, b, j:j + 1], wide[:, blk(j)], ones[:, 0:1], start=True, stop=True)
                last.then_inc(s_col, 1)

            def replicate(first_bank):
                for j in range(C):
                    last = pe.matmul(ps[:, first_bank + j // 4, blk(j % 4)], ones[:, :], wide[:, blk(j)],
                                     start=True, stop=True)
                last.then_inc(s_rep, 1)

            pe.wait_ge(s_kept, KEPT)
            pe.wait_ge(s_sq, 1)
            column_sums(2)
            pe.wait_ge(s_diag, 1)
            replicate(4)
            pe.wait_ge(s_unit, 1)
            for i in range(C):
                if i >= 3:
                    pe.wait_ge(s_sim, i - 2)
                for f in range(2):
                    last = pe.matmul(ps[:, PSUM3[i % 3] + f, :], hsum[:, blk(i)], hsum[:, half(f)],
                                     start=True, stop=True)
                last.then_inc(s_dot, 1)
            pe.wait_ge(s_adj, C)
            for i in range(C):
                if i >= 2:
                    pe.wait_ge(s_sym, i - 1)
                for j in range(C):
                    last = pe.transpose(ps[:, 4 + i % 2, :].bitcast(BF16)[:, blk(j)], adj[:, j, blk(i)], identb[:, :])
                last.then_inc(s_tr, 1)
            for i in range(C):
                if i >= 3:
                    pe.wait_ge(s_csq, i - 2)
                for k in range(C):
                    if i == 0:
                        pe.wait_ge(s_nm, k + 1)
                    for f in range(2):
                        last = pe.matmul(ps[:, PSUM3[i % 3] + f, :], nmask[:, k, blk(i)], nmask[:, k, half(f)],
                                         start=k == 0, stop=k == C - 1)
                last.then_inc(s_com, 1)
            pe.wait_ge(s_colsum, C - 1)
            column_sums(4)
            pe.wait_ge(s_diag, 2)
            replicate(6)

            def second(q):
                for j in range(GROUP):
                    n = q * GROUP + j
                    pe.wait_ge(s_xw, n + 1)
                    if 1 <= j < GROUP - 1:
                        pe.wait_ge(s_h2, q * (GROUP - 2) + j)
                        times_weight(h2[:, (j + 1) % 2, :], 4).then_inc(s_hw2, 1)
                    wait(pe, s_res, n - 1)
                    for c in range(C):
                        if isinstance(q, int) and j == 0:
                            pe.wait_ge(s_wn, c + 1)
                        for f in range(2):
                            last = pe.matmul(ps[:, 2 * (j % 2) + f, :], xw[:, j % 2, c, :], graph[:, c, half(f)],
                                             start=c == 0, stop=c == C - 1)
                    last.then_inc(s_mm, 1)

            rounds(pe, ROUNDS, second)


_INS = ["x", "adj", "L0_gnn_bias", "L0_gnn_gumbel"]


def kernel(**inputs):
    import numpy as _np
    import concourse.bacc as _bacc
    from concourse import mybir as _mybir
    from concourse.bass_utils import run_bass_kernel_spmd as _run

    nc = _bacc.Bacc("TRN2", target_bir_lowering=False, num_devices=1)
    arrays, args = {}, []
    for name in _INS:
        a = _np.ascontiguousarray(inputs[name])
        arrays[f"in_{name}"] = a
        args.append(nc.dram_tensor(f"in_{name}", a.shape, _mybir.dt.from_np(a.dtype), kind="ExternalInput").ap())
    shape = arrays["in_x"].shape
    args.append(nc.dram_tensor("out_0", shape, FP32, kind="ExternalOutput").ap())
    gnn_kernel(nc, *args)
    r = _run(nc, [arrays], core_ids=[0])
    return r.results[0]["out_0"]
```

```python
from contextlib import ExitStack

import concourse.bass as bass
from concourse import mybir

FP32 = mybir.dt.float32
BF16 = mybir.dt.bfloat16
ALU = mybir.AluOpType
ACT = mybir.ActivationFunctionType
AX_X = mybir.AxisListType.X
RMAX = bass.bass_isa.ReduceOp.max


def gnn_kernel(nc, x, weight, bias, gumbel, out):
    B, T, N = x.shape
    C = N // 128
    HALF = 512
    PAIRS = B // 2
    EPS = 1e-5
    GROUP = 4
    ROUNDS = PAIRS // GROUP
    KEPT = 2 * ROUNDS
    XPAIRS = 8
    PROD = 7
    FOLD = 6

    gum = gumbel.rearrange("(c p d) k -> c p (d k)", c=C, p=128)
    bias_col = bias.rearrange("(p a) -> p a", a=1)

    ctx = ExitStack()
    with ctx:
        def sb(name, shape, dt=FP32):
            return ctx.enter_context(nc.sbuf_tensor(name, shape, dt))

        def sem(name):
            return ctx.enter_context(nc.semaphore(name))

        ident = sb("ident", [128, 128])
        identb = sb("identb", [128, 128], BF16)
        ones = sb("ones", [128, 128])
        w_sb = sb("w_sb", [128, T])
        bias_sb = sb("bias_sb", [128, 1])
        eps_sb = sb("eps_sb", [128, 1])
        rstd = sb("rstd", [128, B])
        shift = sb("shift", [128, B])
        stats = sb("stats", [128, 2, 2, 12])
        mv = sb("mv", [128, 2, 2, 2])
        small = sb("small", [128, 2, 6, 2])
        node = sb("node", [128, 10, C])
        dmax = sb("dmax", [128, 4])
        hsum = sb("hsum", [128, N])
        wide = sb("wide", [128, N])
        kept = sb("kept", [128, KEPT, N])

        region1 = sb("region1", [128, XPAIRS * 2 * N])
        xin = region1[:, :].rearrange("p (s b n) -> p s b n", s=XPAIRS, b=2)
        sim = region1[:, 0:4 * N].rearrange("p (s n) -> p s n", s=4)
        dis = region1[:, 4 * N:8 * N].rearrange("p (s n) -> p s n", s=4)
        graph = region1[:, 0:C * N].rearrange("p (c n) -> p c n", c=C)
        squares = region1[:, C * N:(C + 2) * N].rearrange("p (s n) -> p s n", s=2)
        masks = region1[:, (C + 2) * N:(C + 3) * N].bitcast(BF16).rearrange("p (s n) -> p s n", s=2)
        KC = C // 2
        b11, b21 = graph[:, 0:KC, 0:HALF], graph[:, KC:C, 0:HALF]
        b12, b22 = graph[:, 0:KC, HALF:N], graph[:, KC:C, HALF:N]
        t1 = b12
        t2, t3, t4 = (region1[:, C * N + f * KC * HALF:C * N + (f + 1) * KC * HALF].rearrange("p (c n) -> p c n", c=KC)
                      for f in range(3))
        region2 = sb("region2", [128, 16 * N])
        h1 = region2[:, 0:4 * N].rearrange("p (s n) -> p s n", s=4)
        adj = region2[:, 8 * N:12 * N].bitcast(BF16).rearrange("p (c n) -> p c n", c=C)
        nmask = region2[:, 12 * N:16 * N].bitcast(BF16).rearrange("p (c n) -> p c n", c=C)
        gin = [region2[:, f * N:(f + 2) * N].rearrange("p (n k) -> p n k", k=2) for f in (4, 6, 12, 14, 0, 2)]
        GSLOTS = len(gin)
        x2 = region2[:, 0:4 * N].rearrange("p (s b n) -> p s b n", s=2, b=2)
        h2 = region2[:, 4 * N:6 * N].rearrange("p (b n) -> p b n", b=2)
        xw = region2[:, 6 * N:10 * N].rearrange("p (s b c o) -> p s b c o", s=2, b=2, c=C)
        sums = region2[:, 10 * N:14 * N].rearrange("p (s k c o) -> p s k c o", s=2, k=4, c=KC)
        fold = wide[:, :].rearrange("p (k n) -> p k n", k=2)
        fold3 = hsum[:, 0:HALF]

        ps = ctx.enter_context(nc.psum_tensor("ps", [128, 8, HALF], FP32))

        def bank(k, n=1):
            return ps[:, k:k + n, :].rearrange("p k n -> p (k n)")

        s_const = sem("s_const")
        s_in = sem("s_in")
        s_x = [sem(f"s_x{k}") for k in range(XPAIRS)]
        s_bn = sem("s_bn")
        s_mv = sem("s_mv")
        s_std = sem("s_std")
        s_newton = sem("s_newton")
        s_row = sem("s_row")
        s_h = sem("s_h")
        s_even = sem("s_even")
        s_odd = sem("s_odd")
        s_hw = sem("s_hw")
        s_kept = sem("s_kept")
        s_dve = sem("s_dve")
        s_sum = sem("s_sum")
        s_sq = sem("s_sq")
        s_col = sem("s_col")
        s_guard = sem("s_guard")
        s_root = sem("s_root")
        s_diag = sem("s_diag")
        s_rep = sem("s_rep")
        s_unit = sem("s_unit")
        s_g = [sem(f"s_g{k}") for k in range(GSLOTS)]
        s_dot = sem("s_dot")
        s_sim = sem("s_sim")
        s_dis = sem("s_dis")
        s_score0 = sem("s_score0")
        s_score1 = sem("s_score1")
        s_adj = sem("s_adj")
        s_tr = sem("s_tr")
        s_sym = sem("s_sym")
        s_nm = sem("s_nm")
        s_cnt = sem("s_cnt")
        s_pmax = sem("s_pmax")
        s_gmax = sem("s_gmax")
        s_com = sem("s_com")
        s_csq = sem("s_csq")
        s_mask = sem("s_mask")
        s_edge = sem("s_edge")
        s_colsum = sem("s_colsum")
        s_wn = sem("s_wn")
        s_half = sem("s_half")
        s_x2 = [sem(f"s_x2{k}") for k in range(2)]
        s_h2 = sem("s_h2")
        s_hw2 = sem("s_hw2")
        s_xw = sem("s_xw")
        s_comb = sem("s_comb")
        s_prod = sem("s_prod")
        s_p1 = sem("s_p1")
        s_fold = sem("s_fold")
        s_y = sem("s_y")
        s_st = [sem(f"s_st{k}") for k in range(2)]
        block = ctx.enter_context(nc.Block())

        def wait(eng, s, value):
            if not isinstance(value, int) or value > 0:
                eng.wait_ge(s, value)

        def rounds_to_last(eng, count, body):
            body(0)
            with eng.Fori(1, count - 1) as r:
                body(r)
            body(count - 1)

        def rounds(eng, count, body):
            body(0)
            with eng.Fori(1, count) as r:
                body(r)

        def blk(j):
            return slice(128 * j, 128 * j + 128)

        def half(j):
            return slice(HALF * j, HALF * j + HALF)

        PSUM3 = (0, 2, 6)

        @block.sync
        def _(sp):
            sp.dma_start(w_sb[:, :], weight).then_inc(s_in, 16)
            sp.dma_start(bias_sb[:, :], bias_col).then_inc(s_in, 16)

            def load_pairs(r):
                for k in range(XPAIRS):
                    wait(sp, s_h, (r - 1) * (2 * XPAIRS) + 2 * k + 2)
                    sp.dma_start(xin[:, k, :, :],
                                 x[bass.ds(r * (2 * XPAIRS) + 2 * k, 2), :, :].rearrange("b t n -> t b n")
                                 ).then_inc(s_x[k], 16)

            rounds(sp, PAIRS // XPAIRS, load_pairs)
            for i in range(C):
                if 4 <= i < GSLOTS:
                    sp.wait_ge(s_even, PAIRS)
                    sp.wait_ge(s_odd, PAIRS)
                if i >= GSLOTS:
                    sp.wait_ge(s_adj, i - GSLOTS + 1)
                sp.dma_start(gin[i % GSLOTS].rearrange("p n k -> p (n k)"), gum[i, :, :]).then_inc(s_g[i % GSLOTS], 16)
            sp.wait_ge(s_adj, C)

            def load_pair(k, pair):
                sp.dma_start(x2[:, k % 2, :, :], x[bass.ds(pair * 2, 2), :, :].rearrange("b t n -> t b n")
                             ).then_inc(s_x2[k % 2], 16)

            load_pair(0, 0)
            load_pair(1, 1)

            def stores(q):
                for k in range(GROUP):
                    pair = q * GROUP + k
                    for b in (1, 0):
                        sp.wait_ge(s_fold, pair * FOLD + (FOLD - b))
                        sp.dma_start(out[bass.ds(pair * 2 + b, 1), :, :].rearrange("a t n -> t (a n)"),
                                     x2[:, k % 2, b, :]).then_inc(s_st[k % 2], 16)
                    if not (isinstance(q, int) and q == ROUNDS - 1 and k >= GROUP - 2):
                        sp.wait_ge(s_st[k % 2], q * (GROUP * 16) + (k // 2 + 1) * 32)
                        load_pair(k, pair + 2)

            rounds_to_last(sp, ROUNDS, stores)
            for slot in range(2):
                sp.wait_ge(s_st[slot], 16 * PAIRS)

        @block.gpsimd
        def _(pool):
            pool.memset(ones[:, :], 1.0).then_inc(s_const, 1)
            pool.memset(eps_sb[:, :], EPS).then_inc(s_const, 1)
            pool.memset(hsum[:, :], 0.0).then_inc(s_const, 1)
            pool.wait_ge(s_const, 3)
            pool.affine_select(out=ident[:, :], in_=ones[:, :], compare_op=ALU.is_equal, fill=0.0, base=0,
                               pattern=[[-1, 128]], channel_multiplier=1).then_inc(s_const, 1)
            pool.wait_ge(s_const, 4)
            pool.tensor_copy(identb[:, :], ident[:, :]).then_inc(s_const, 1)

            def add_even(r):
                for k in range(XPAIRS):
                    pair = r * XPAIRS + k
                    pool.wait_ge(s_h, pair * 2 + 1)
                    wait(pool, s_even, pair)
                    pool.tensor_tensor(hsum[:, :], hsum[:, :], h1[:, 2 * (k % 2), :], ALU.add).then_inc(s_even, 1)

            rounds(pool, PAIRS // XPAIRS, add_even)

            for i in range(C):
                pool.wait_ge(s_dis, i + 1)
                pool.wait_ge(s_g[i % GSLOTS], 16 * (i // GSLOTS + 1))
                pool.tensor_tensor(dis[:, i % 4, :], dis[:, i % 4, :], gin[i % GSLOTS][:, :, 1], ALU.add
                                   ).then_inc(s_score1, 1)
            pool.wait_ge(s_pmax, 1)
            pool.partition_all_reduce(dmax[:, 1:2], dmax[:, 0:1], 128, RMAX).then_inc(s_gmax, 1)
            for i in range(1, C - 1):
                pool.wait_ge(s_edge, i + 1)
                if i > 1:
                    pool.wait_ge(s_colsum, i - 1)
                pool.tensor_tensor(wide[:, :], graph[:, 0, :] if i == 1 else wide[:, :], graph[:, i, :], ALU.add
                                   ).then_inc(s_colsum, 1)

            def add_x(q):
                for k in range(GROUP):
                    pair, slot = q * GROUP + k, k % 2
                    pool.wait_ge(s_x2[slot], q * (GROUP * 8) + (k // 2 + 1) * 16)
                    for b, f, step, u in ((0, 1, 1, fold[:, 1, :]), (1, 0, 1, fold[:, 1, :]), (1, 1, 2, fold3)):
                        pool.wait_ge(s_fold, pair * FOLD + step)
                        pool.tensor_tensor(x2[:, slot, b, half(f)], x2[:, slot, b, half(f)], u, ALU.add
                                           ).then_inc(s_y, 1)

            rounds(pool, ROUNDS, add_x)

        @block.scalar
        def _(act):
            act.wait_ge(s_const, 2)

            def std(k, pair):
                act.wait_ge(s_mv, pair + 1)
                act.activation(small[:, k % 2, 0, :], mv[:, k % 2, :, 1], ACT.Sqrt, bias=eps_sb[:, :]
                               ).then_inc(s_std, 1)

            def relu(k, pair):
                act.wait_ge(s_row, pair + 1)
                wait(act, s_even, pair - 1)
                wait(act, s_odd, pair - 1)
                for b in range(2):
                    n = pair * 2 + b
                    act.activation(h1[:, 2 * (k % 2) + b, :], xin[:, k % XPAIRS, b, :], ACT.Relu,
                                   bias=shift[:, bass.ds(n, 1)], scale=rstd[:, bass.ds(n, 1)]).then_inc(s_h, 1)

            def first(r):
                for k in range(XPAIRS):
                    pair = r * XPAIRS + k
                    std(k, pair)
                    if k or not isinstance(r, int):
                        relu((k - 1) % XPAIRS, pair - 1)
                    if k % 4 == 2:
                        for b in range(2):
                            n = r * 4 + k // 4 * 2 + b
                            act.wait_ge(s_hw, n + 1)
                            act.activation(kept[:, bass.ds(n, 1), :], bank(2 + 2 * b, 2).rearrange("p (a n) -> p a n", a=1),
                                           ACT.Copy).then_inc(s_kept, 1)

            rounds(act, PAIRS // XPAIRS, first)
            relu(XPAIRS - 1, PAIRS - 1)

            act.wait_ge(s_sum, 1)
            act.activation(wide[:, :], hsum[:, :], ACT.Square, scale=1.0 / B).then_inc(s_sq, 1)
            act.wait_ge(s_guard, 1)
            act.activation(node[:, 1, :], node[:, 0, :], ACT.Sqrt).then_inc(s_root, 1)
            for i in range(C):
                act.wait_ge(s_dot, i + 1)
                if i >= 4:
                    act.wait_ge(s_adj, i - 3)
                act.activation(sim[:, i % 4, :], bank(PSUM3[i % 3], 2), ACT.Copy, scale=0.5, bias=0.5
                               ).then_inc(s_sim, 1)
                act.wait_ge(s_sim, i + 1)
                act.activation(dis[:, i % 4, :], sim[:, i % 4, :], ACT.Copy, scale=-1.0, bias=1.0).then_inc(s_dis, 1)
            for i in range(C):
                act.wait_ge(s_nm, i + 1)
                if i >= 2:
                    act.wait_ge(s_cnt, i - 1)
                act.activation(squares[:, i % 2, :], nmask[:, i, :], ACT.Copy, accum_out=node[:, 6, i:i + 1]
                               ).then_inc(s_cnt, 1)
            act.wait_ge(s_cnt, C)
            for i in range(C):
                act.wait_ge(s_com, i + 1)
                if i >= 2:
                    act.wait_ge(s_edge, i - 1)
                act.activation(squares[:, i % 2, :], bank(PSUM3[i % 3], 2), ACT.Square).then_inc(s_csq, 1)

            def take(k, q):
                for b in range(2):
                    to = xw[:, k % 2, b, :, :].rearrange("p c o -> p (c o)")
                    if k == 0:
                        act.activation(to.rearrange("p (a n) -> p a n", a=1), kept[:, bass.ds(q * 2 + b, 1), :],
                                       ACT.Copy).then_inc(s_xw, 1)
                    else:
                        act.wait_ge(s_hw2, q * (2 * GROUP - 2) + 2 * k + b - 1)
                        act.activation(to, bank(4 + 2 * b, 2), ACT.Copy).then_inc(s_xw, 1)

            act.wait_ge(s_adj, C)
            take(0, 0)
            act.wait_ge(s_guard, 2)
            act.activation(node[:, 1, :], node[:, 0, :], ACT.Sqrt).then_inc(s_root, 1)

            def second(q):
                for k in range(GROUP):
                    pair = q * GROUP + k
                    act.wait_ge(s_prod, pair * PROD + 1)
                    wait(act, s_fold, pair * FOLD - FOLD + 1)
                    act.activation(fold[:, 0, :], ps[:, 0, :], ACT.Identity, bias=bias_sb[:, :]).then_inc(s_p1, 1)
                    if k + 1 < GROUP:
                        act.wait_ge(s_x2[(k + 1) % 2], q * (GROUP * 8) + ((k + 1) // 2 + 1) * 16)
                        wait(act, s_hw2, q * (2 * GROUP - 2) + 2 * k)
                        for b in range(2):
                            n = pair * 2 + 2 + b
                            act.activation(h2[:, b, :], x2[:, (k + 1) % 2, b, :], ACT.Relu,
                                           bias=shift[:, bass.ds(n, 1)], scale=rstd[:, bass.ds(n, 1)]
                                           ).then_inc(s_h2, 1)
                    if k + 1 < GROUP:
                        take(k + 1, q)
                    elif not (isinstance(q, int) and q == ROUNDS - 1):
                        take(0, q + 1)

            rounds_to_last(act, ROUNDS, second)

        @block.vector
        def _(dve):
            dve.wait_ge(s_const, 5)
            dve.wait_ge(s_in, 32)

            def newton(k, pair):
                root, inv, inv2, t, u = (small[:, k % 2, c, :] for c in range(5))
                mean, var = mv[:, k % 2, :, 0], mv[:, k % 2, :, 1]
                here = bass.ds(pair * 2, 2)
                dve.wait_ge(s_std, pair + 1)
                dve.reciprocal(inv, root).then_inc(s_newton, 1)
                yield
                dve.wait_ge(s_newton, pair * 5 + 1)
                dve.tensor_tensor(inv2, inv, inv, ALU.mult).then_inc(s_newton, 1)
                yield
                dve.wait_ge(s_newton, pair * 5 + 2)
                dve.scalar_tensor_tensor(out=t, in0=var, scalar=EPS, in1=inv2, op0=ALU.add, op1=ALU.mult
                                         ).then_inc(s_newton, 1)
                yield
                dve.wait_ge(s_newton, pair * 5 + 3)
                dve.tensor_scalar(u, t, -0.5, 1.5, ALU.mult, ALU.add).then_inc(s_newton, 1)
                yield
                dve.wait_ge(s_newton, pair * 5 + 4)
                dve.tensor_tensor(rstd[:, here], u, inv, ALU.mult).then_inc(s_newton, 1)
                dve.wait_ge(s_newton, pair * 5 + 5)
                dve.scalar_tensor_tensor(out=shift[:, here], in0=mean, scalar=-1.0, in1=rstd[:, here],
                                         op0=ALU.mult, op1=ALU.mult).then_inc(s_row, 1)
                yield

            def first(r):
                for k in range(XPAIRS):
                    pair = r * XPAIRS + k
                    before = newton((k - 1) % XPAIRS, pair - 1) if k or not isinstance(r, int) else iter(())
                    dve.wait_ge(s_x[k], (r + 1) * 16)
                    for b in range(2):
                        for f in range(2):
                            last = dve.bn_stats(stats[:, k % 2, b, 6 * f:6 * f + 6], xin[:, k, b, half(f)])
                            if b == f == 1:
                                last.then_inc(s_bn, 1)
                                dve.wait_ge(s_bn, pair + 1)
                            next(before, None)
                    next(before, None)
                    for b in range(2):
                        last = dve.bn_aggr(mv[:, k % 2, b, :], stats[:, k % 2, b, :])
                    last.then_inc(s_mv, 1)

            rounds(dve, PAIRS // XPAIRS, first)
            for _ in newton(XPAIRS - 1, PAIRS - 1):
                pass

            chain = [0]

            def step(ins):
                chain[0] += 1
                ins.then_inc(s_dve, 1)
                dve.wait_ge(s_dve, chain[0])

            def inverse_root(n, scale):
                dve.wait_ge(s_root, n)
                step(dve.reciprocal(node[:, 2, :], node[:, 1, :]))
                step(dve.tensor_tensor(node[:, 3, :], node[:, 2, :], node[:, 2, :], ALU.mult))
                step(dve.tensor_tensor(node[:, 4, :], node[:, 3, :], node[:, 0, :], ALU.mult))
                step(dve.tensor_scalar(node[:, 3, :], node[:, 4, :], -0.5, 1.5, ALU.mult, ALU.add))
                step(dve.scalar_tensor_tensor(out=node[:, 5, :], in0=node[:, 3, :], scalar=scale, in1=node[:, 2, :],
                                              op0=ALU.mult, op1=ALU.mult))

            def diagonal():
                for j in range(C):
                    last = dve.tensor_scalar(wide[:, blk(j)], ident[:, :], node[:, 5, j:j + 1], None, ALU.mult)
                last.then_inc(s_diag, 1)

            dve.wait_ge(s_odd, PAIRS)
            dve.wait_ge(s_even, PAIRS)
            dve.tensor_tensor(hsum[:, :], bank(0, 2), hsum[:, :], ALU.add).then_inc(s_sum, 1)
            dve.wait_ge(s_col, 1)
            dve.tensor_scalar(node[:, 0, :], ps[:, 2, 0:C], 1e-24, None, ALU.max).then_inc(s_guard, 1)
            inverse_root(1, 1.0 / B)
            diagonal()
            dve.wait_ge(s_rep, 1)
            dve.tensor_tensor(hsum[:, :], bank(4, 2), hsum[:, :], ALU.mult).then_inc(s_unit, 1)

            def score0(i):
                dve.wait_ge(s_dis, i + 1)
                dve.wait_ge(s_g[i % GSLOTS], 16 * (i // GSLOTS + 1))
                dve.tensor_tensor(sim[:, i % 4, :], sim[:, i % 4, :], gin[i % GSLOTS][:, :, 0], ALU.add
                                  ).then_inc(s_score0, 1)

            score0(0)
            for i in range(C):
                if i + 1 < C:
                    score0(i + 1)
                dve.wait_ge(s_score0, i + 1)
                dve.wait_ge(s_score1, i + 1)
                dve.tensor_tensor(adj[:, i, :], sim[:, i % 4, :], dis[:, i % 4, :], ALU.is_gt).then_inc(s_adj, 1)
            for i in range(C):
                dve.wait_ge(s_tr, i + 1)
                dve.tensor_tensor(nmask[:, i, :], ps[:, 4 + i % 2, :].bitcast(BF16), adj[:, i, :], ALU.max
                                  ).then_inc(s_sym, 1)
                dve.wait_ge(s_sym, i + 1)
                dve.tensor_tensor(nmask[:, i, blk(i)], nmask[:, i, blk(i)], identb[:, :], ALU.max).then_inc(s_nm, 1)
            dve.wait_ge(s_cnt, C)
            dve.reduce_max(dmax[:, 0:1], node[:, 6, :], AX_X).then_inc(s_pmax, 1)

            def mask(i):
                dve.wait_ge(s_csq, i + 1)
                dve.scalar_tensor_tensor(out=masks[:, i % 2, 0:N], in0=squares[:, i % 2, :], scalar=1.0,
                                         in1=adj[:, i, :], op0=ALU.is_gt, op1=ALU.mult).then_inc(s_mask, 1)

            mask(0)
            for i in range(C):
                if i + 1 < C:
                    mask(i + 1)
                dve.wait_ge(s_mask, i + 1)
                dve.tensor_tensor(graph[:, i, :], squares[:, i % 2, :], masks[:, i % 2, 0:N], ALU.mult
                                  ).then_inc(s_edge, 1)

            dve.wait_ge(s_gmax, 1)
            step(dve.reciprocal(dmax[:, 2:3], dmax[:, 1:2]))
            dve.wait_ge(s_col, 2)
            step(dve.tensor_scalar(node[:, 7, :], ps[:, 4, 0:C], dmax[:, 2:3], None, ALU.mult))
            dve.tensor_scalar(node[:, 0, :], node[:, 7, :], 1e-6, None, ALU.max).then_inc(s_guard, 1)
            step(dve.tensor_scalar(node[:, 8, :], node[:, 7, :], 0.0, None, ALU.is_gt))
            inverse_root(2, 1.0)
            step(dve.tensor_tensor(node[:, 5, :], node[:, 5, :], node[:, 8, :], ALU.mult))
            dve.tensor_scalar(node[:, 9, :], node[:, 5, :], dmax[:, 2:3], None, ALU.mult)
            diagonal()
            dve.wait_ge(s_diag, 2)
            dve.wait_ge(s_rep, 2)
            for f, first_chunk in ((0, 0), (1, 0), (1, KC), (0, KC)):
                for i in range(first_chunk, first_chunk + KC):
                    dve.scalar_tensor_tensor(out=graph[:, i, half(f)], in0=graph[:, i, half(f)],
                                             scalar=node[:, 9, i:i + 1], in1=ps[:, 6 + f, :],
                                             op0=ALU.mult, op1=ALU.mult).then_inc(s_wn, 1)
                if (f, first_chunk) == (1, KC):
                    dve.wait_ge(s_wn, 3 * KC)
                    dve.tensor_tensor(t3, b22, b12, ALU.subtract).then_inc(s_half, 1)
                    dve.wait_ge(s_half, 1)
                    dve.tensor_tensor(t1, b12, b11, ALU.subtract).then_inc(s_half, 1)
                    dve.wait_ge(s_half, 2)
                    dve.tensor_tensor(t2, b22, t1, ALU.subtract).then_inc(s_half, 1)
            dve.wait_ge(s_wn, 4 * KC)
            dve.wait_ge(s_half, 3)
            dve.tensor_tensor(t4, b21, t2, ALU.subtract).then_inc(s_half, 1)

            def combine(k, pair):
                a11, a12 = xw[:, k % 2, 0, 0:KC, :], xw[:, k % 2, 0, KC:C, :]
                a21, a22 = xw[:, k % 2, 1, 0:KC, :], xw[:, k % 2, 1, KC:C, :]
                s1, s2, s3, s4 = (sums[:, k % 2, c, :, :] for c in range(4))
                dve.wait_ge(s_xw, pair * 2 + 2)
                dve.tensor_tensor(s1, a21, a22, ALU.add).then_inc(s_comb, 1)
                dve.tensor_tensor(s3, a11, a21, ALU.subtract).then_inc(s_comb, 1)
                dve.wait_ge(s_comb, pair * 4 + 1)
                dve.tensor_tensor(s2, s1, a11, ALU.subtract).then_inc(s_comb, 1)
                dve.wait_ge(s_comb, pair * 4 + 3)
                dve.tensor_tensor(s4, a12, s2, ALU.subtract).then_inc(s_comb, 1)

            def second(q):
                for k in range(GROUP):
                    pair, slot = q * GROUP + k, k % 2
                    bank_a, bank_b, bank_c, bank_d = (ps[:, c, :] for c in range(4))
                    u2 = fold[:, 1, :]
                    dve.wait_ge(s_p1, pair + 1)
                    dve.wait_ge(s_prod, pair * PROD + 2)
                    wait(dve, s_y, pair * 3 - 1)
                    dve.tensor_tensor(u2, bank_b, fold[:, 0, :], ALU.add).then_inc(s_fold, 1)
                    dve.wait_ge(s_prod, pair * PROD + 3)
                    dve.wait_ge(s_fold, pair * FOLD + 1)
                    wait(dve, s_y, pair * 3)
                    dve.tensor_tensor(fold3, bank_c, u2, ALU.add).then_inc(s_fold, 1)

                    def result(b, f, product, bank_):
                        dve.wait_ge(s_prod, pair * PROD + product)
                        dve.tensor_tensor(x2[:, slot, b, half(f)], bank_, x2[:, slot, b, half(f)], ALU.add
                                          ).then_inc(s_fold, 1)

                    dve.wait_ge(s_y, pair * 3 + 3)
                    result(1, 1, 4, bank_d)
                    dve.wait_ge(s_prod, pair * PROD + 5)
                    dve.scalar_tensor_tensor(out=x2[:, slot, 0, half(0)], in0=bank_a, scalar=bias_sb[:, :],
                                             in1=x2[:, slot, 0, half(0)], op0=ALU.add, op1=ALU.add
                                             ).then_inc(s_fold, 1)
                    if k + 1 < GROUP:
                        combine(k + 1, pair + 1)
                    elif not (isinstance(q, int) and q == ROUNDS - 1):
                        combine(0, pair + 1)
                    result(1, 0, 6, bank_c)
                    result(0, 1, 7, bank_d)

            combine(0, 0)
            rounds_to_last(dve, ROUNDS, second)

        @block.tensor
        def _(pe):
            pe.wait_ge(s_const, 5)
            pe.wait_ge(s_in, 32)

            def times_weight(h, first_bank):
                for c in range(C):
                    last = pe.matmul(ps[:, first_bank + c // 4, blk(c % 4)], h[:, blk(c)], w_sb[:, :],
                                     start=True, stop=True)
                return last

            def first(r):
                for k in range(XPAIRS):
                    pair = r * XPAIRS + k
                    if k % 4 == 0:
                        for b in range(2):
                            n = r * 4 + k // 4 * 2 + b
                            pe.wait_ge(s_h, pair * 2 + b + 1)
                            wait(pe, s_kept, n - 1)
                            times_weight(h1[:, 2 * (k % 2) + b, :], 2 + 2 * b).then_inc(s_hw, 1)
                    pe.wait_ge(s_h, pair * 2 + 2)
                    for f in range(2):
                        last = pe.matmul(ps[:, f, :], ident[:, :], h1[:, 2 * (k % 2) + 1, half(f)],
                                         start=isinstance(r, int) and k == 0, stop=True, skip_group_check=True)
                    last.then_inc(s_odd, 1)

            rounds(pe, PAIRS // XPAIRS, first)

            def column_sums(b):
                for j in range(C):
                    last = pe.matmul(ps[:, b, j:j + 1], wide[:, blk(j)], ones[:, 0:1], start=True, stop=True)
                last.then_inc(s_col, 1)

            def replicate(first_bank):
                for j in range(C):
                    last = pe.matmul(ps[:, first_bank + j // 4, blk(j % 4)], ones[:, :], wide[:, blk(j)],
                                     start=True, stop=True)
                last.then_inc(s_rep, 1)

            pe.wait_ge(s_kept, KEPT)
            pe.wait_ge(s_sq, 1)
            column_sums(2)
            pe.wait_ge(s_diag, 1)
            replicate(4)
            pe.wait_ge(s_unit, 1)
            for i in range(C):
                if i >= 3:
                    pe.wait_ge(s_sim, i - 2)
                for f in range(2):
                    last = pe.matmul(ps[:, PSUM3[i % 3] + f, :], hsum[:, blk(i)], hsum[:, half(f)],
                                     start=True, stop=True)
                last.then_inc(s_dot, 1)
            pe.wait_ge(s_adj, C)
            for i in range(C):
                if i >= 2:
                    pe.wait_ge(s_sym, i - 1)
                for j in range(C):
                    last = pe.transpose(ps[:, 4 + i % 2, :].bitcast(BF16)[:, blk(j)], adj[:, j, blk(i)], identb[:, :])
                last.then_inc(s_tr, 1)
            for i in range(C):
                if i >= 3:
                    pe.wait_ge(s_csq, i - 2)
                for k in range(C):
                    if i == 0:
                        pe.wait_ge(s_nm, k + 1)
                    for f in range(2):
                        last = pe.matmul(ps[:, PSUM3[i % 3] + f, :], nmask[:, k, blk(i)], nmask[:, k, half(f)],
                                         start=k == 0, stop=k == C - 1)
                last.then_inc(s_com, 1)
            pe.wait_ge(s_colsum, C - 2)
            for j in range(C):
                pe.matmul(ps[:, 4, j:j + 1], wide[:, blk(j)], ones[:, 0:1], start=j == 0, stop=True,
                          skip_group_check=True)
            pe.wait_ge(s_edge, C)
            for j in range(C):
                last = pe.matmul(ps[:, 4, j:j + 1], graph[:, C - 1, blk(j)], ones[:, 0:1], start=False, stop=True,
                                 skip_group_check=True)
            last.then_inc(s_col, 1)
            pe.wait_ge(s_diag, 2)
            replicate(6)

            def product(a, b_, bank_, onto):
                for c in range(KC):
                    last = pe.matmul(ps[:, bank_, :], a[:, c, :], b_[:, c, :], start=not onto and c == 0,
                                     stop=c == KC - 1, skip_group_check=True)
                last.then_inc(s_prod, 1)

            def second(q):
                for k in range(GROUP):
                    pair, slot = q * GROUP + k, k % 2
                    start = isinstance(q, int) and q == 0 and k == 0
                    a11, a12, a22 = (xw[:, slot, b, c:c + KC, :] for b, c in ((0, 0), (0, KC), (1, KC)))
                    s1, s2, s3, s4 = (sums[:, slot, c, :, :] for c in range(4))
                    pe.wait_ge(s_xw, pair * 2 + 2)
                    if start:
                        pe.wait_ge(s_wn, KC)
                    wait(pe, s_fold, pair * FOLD - 2)
                    product(a11, b11, 0, False)
                    pe.wait_ge(s_comb, pair * 4 + 4)
                    if start:
                        pe.wait_ge(s_half, 3)
                    product(s2, t2, 1, False)
                    wait(pe, s_fold, pair * FOLD - 1)
                    product(s3, t3, 2, False)
                    if k + 1 < GROUP:
                        if start:
                            pe.wait_ge(s_wn, 4 * KC)
                        for b in range(2):
                            pe.wait_ge(s_h2, q * (2 * GROUP - 2) + 2 * k + b + 1)
                            times_weight(h2[:, b, :], 4 + 2 * b).then_inc(s_hw2, 1)
                    wait(pe, s_fold, pair * FOLD)
                    product(s1, t1, 3, False)
                    pe.wait_ge(s_p1, pair + 1)
                    if start:
                        pe.wait_ge(s_wn, 4 * KC)
                    product(a12, b21, 0, True)
                    pe.wait_ge(s_fold, pair * FOLD + 2)
                    if start:
                        pe.wait_ge(s_half, 4)
                    product(a22, t4, 2, True)
                    pe.wait_ge(s_fold, pair * FOLD + 3)
                    product(s4, b22, 3, True)

            rounds_to_last(pe, ROUNDS, second)


_INS = ["x", "adj", "L0_gnn_bias", "L0_gnn_gumbel"]


def kernel(**inputs):
    import numpy as _np
    import concourse.bacc as _bacc
    from concourse import mybir as _mybir
    from concourse.bass_utils import run_bass_kernel_spmd as _run

    nc = _bacc.Bacc("TRN2", target_bir_lowering=False, num_devices=1)
    arrays, args = {}, []
    for name in _INS:
        a = _np.ascontiguousarray(inputs[name])
        arrays[f"in_{name}"] = a
        args.append(nc.dram_tensor(f"in_{name}", a.shape, _mybir.dt.from_np(a.dtype), kind="ExternalInput").ap())
    shape = arrays["in_x"].shape
    args.append(nc.dram_tensor("out_0", shape, FP32, kind="ExternalOutput").ap())
    gnn_kernel(nc, *args)
    r = _run(nc, [arrays], core_ids=[0])
    return r.results[0]["out_0"]
```

```python
from contextlib import ExitStack

import concourse.bass as bass
from concourse import mybir

FP32 = mybir.dt.float32
BF16 = mybir.dt.bfloat16
FP16 = mybir.dt.float16
ALU = mybir.AluOpType
ACT = mybir.ActivationFunctionType
AX_X = mybir.AxisListType.X
RMAX = bass.bass_isa.ReduceOp.max


def gnn_kernel(nc, x, weight, bias, gumbel, out):
    B, T, N = x.shape
    C = N // 128
    HALF = 512
    PAIRS = B // 2
    EPS = 1e-5
    GROUP = 4
    ROUNDS = PAIRS // GROUP
    KEPT = 2 * ROUNDS
    XPAIRS = 8
    HPAIRS = 4
    PROD = 7
    FOLD = 6

    gum = gumbel.rearrange("(c p d) k -> c p (d k)", c=C, p=128)
    bias_col = bias.rearrange("(p a) -> p a", a=1)

    ctx = ExitStack()
    with ctx:
        def sb(name, shape, dt=FP32):
            return ctx.enter_context(nc.sbuf_tensor(name, shape, dt))

        def sem(name):
            return ctx.enter_context(nc.semaphore(name))

        ident = sb("ident", [128, 128])
        identb = sb("identb", [128, 128], BF16)
        identh = sb("identh", [128, 128], FP16)
        ones = sb("ones", [128, 128])
        w_sb = sb("w_sb", [128, T])
        bias_sb = sb("bias_sb", [128, 1])
        eps_sb = sb("eps_sb", [128, 1])
        rstd = sb("rstd", [128, B])
        shift = sb("shift", [128, B])
        stats = sb("stats", [128, 2, 2, 12])
        mv = sb("mv", [128, 4, 2, 2])
        small = sb("small", [128, 4, 4, 2])
        node = sb("node", [128, 10, C])
        dmax = sb("dmax", [128, 4])
        hsum = sb("hsum", [128, N])
        wide = sb("wide", [128, N])
        kept = sb("kept", [128, KEPT, N])

        region1 = sb("region1", [128, XPAIRS * 2 * N])
        xin = region1[:, :].rearrange("p (s b n) -> p s b n", s=XPAIRS, b=2)
        above = region1[:, 0:C * N].rearrange("p (c n) -> p c n", c=C)
        graph = region1[:, 0:C * N].rearrange("p (c n) -> p c n", c=C)
        squares = region1[:, C * N:(C + 2) * N].rearrange("p (s n) -> p s n", s=2)
        right = region1[:, (C + 2) * N:(C + 4) * N].bitcast(FP16)
        RIGHT = [128 * sum(C - 1 - j for j in range(i)) for i in range(C)]
        x_early = region1[:, (C + 2) * N:(C + 4) * N].rearrange("p (b n) -> p b n", b=2)
        KC = C // 2
        b11, b21 = graph[:, 0:KC, 0:HALF], graph[:, KC:C, 0:HALF]
        b12, b22 = graph[:, 0:KC, HALF:N], graph[:, KC:C, HALF:N]
        t1 = b12
        t2, t4 = (region1[:, f * N:(f + 2) * N].rearrange("p (c n) -> p c n", c=KC) for f in (8, 10))
        LATE = 2
        late = region1[:, 12 * N:16 * N].rearrange("p (s b c o) -> p s b c o", s=LATE, b=2, c=C)
        region2 = sb("region2", [128, 16 * N])
        h1 = region2[:, 8 * N:16 * N].rearrange("p (s b n) -> p s b n", s=HPAIRS, b=2)
        adj = region2[:, 8 * N:12 * N].bitcast(BF16).rearrange("p (c n) -> p c n", c=C)
        nmask = region2[:, 12 * N:16 * N].bitcast(BF16).rearrange("p (c n) -> p c n", c=C)
        GSLOTS = 4
        gin = region2[:, 0:GSLOTS * 2 * N].rearrange("p (s n k) -> p s n k", s=GSLOTS, k=2)
        x2 = region2[:, 0:4 * N].rearrange("p (s b n) -> p s b n", s=2, b=2)
        h2 = region2[:, 4 * N:6 * N].rearrange("p (b n) -> p b n", b=2)
        xw = region2[:, 6 * N:10 * N].rearrange("p (s b c o) -> p s b c o", s=2, b=2, c=C)
        sums = region2[:, 10 * N:14 * N].rearrange("p (s k c o) -> p s k c o", s=2, k=4, c=KC)
        t3 = region2[:, 14 * N:16 * N].rearrange("p (c n) -> p c n", c=KC)
        fold = wide[:, :].rearrange("p (k n) -> p k n", k=2)
        fold3 = hsum[:, 0:HALF]
        columns = hsum[:, HALF:N]

        ps = ctx.enter_context(nc.psum_tensor("ps", [128, 8, HALF], FP32))

        def bank(k, n=1):
            return ps[:, k:k + n, :].rearrange("p k n -> p (k n)")

        s_const = sem("s_const")
        s_in = sem("s_in")
        s_x = [sem(f"s_x{k}") for k in range(XPAIRS)]
        s_x_first = sem("s_x_first")
        s_bn = sem("s_bn")
        s_mv = sem("s_mv")
        s_std = sem("s_std")
        s_inv = sem("s_inv")
        s_quot = sem("s_quot")
        s_newton = sem("s_newton")
        s_rstd = sem("s_rstd")
        s_row = sem("s_row")
        s_h = sem("s_h")
        s_even = sem("s_even")
        s_odd = sem("s_odd")
        s_hw = sem("s_hw")
        s_kept = sem("s_kept")
        s_late_hw = sem("s_late_hw")
        s_late = sem("s_late")
        s_dve = sem("s_dve")
        s_sum = sem("s_sum")
        s_sq = sem("s_sq")
        s_col = sem("s_col")
        s_guard = sem("s_guard")
        s_root = sem("s_root")
        s_diag = sem("s_diag")
        s_rep = sem("s_rep")
        s_unit = sem("s_unit")
        s_g = [sem(f"s_g{k}") for k in range(GSLOTS)]
        s_dot = sem("s_dot")
        s_above = sem("s_above")
        s_above2 = sem("s_above2")
        s_adj = sem("s_adj")
        s_tr = sem("s_tr")
        s_sym = sem("s_sym")
        s_nm = sem("s_nm")
        s_cnt = sem("s_cnt")
        s_pmax = sem("s_pmax")
        s_gmax = sem("s_gmax")
        s_com = sem("s_com")
        s_right = sem("s_right")
        s_left = sem("s_left")
        s_csq = sem("s_csq")
        s_lsq = sem("s_lsq")
        s_mask = sem("s_mask")
        s_edge = sem("s_edge")
        s_colsum = sem("s_colsum")
        s_two = sem("s_two")
        s_rows = sem("s_rows")
        s_repc = sem("s_repc")
        s_b21r = sem("s_b21r")
        s_b11 = sem("s_b11")
        s_b2 = sem("s_b2")
        s_t3 = sem("s_t3")
        s_t1 = sem("s_t1")
        s_t2 = sem("s_t2")
        s_b21 = sem("s_b21")
        s_t4 = sem("s_t4")
        s_x2 = [sem(f"s_x2{k}") for k in range(2)]
        s_x_early = sem("s_x_early")
        s_h2 = sem("s_h2")
        s_hw2 = sem("s_hw2")
        s_xw = sem("s_xw")
        s_comb = sem("s_comb")
        s_prod = sem("s_prod")
        s_p1 = sem("s_p1")
        s_fold = sem("s_fold")
        s_y = sem("s_y")
        s_st = [sem(f"s_st{k}") for k in range(2)]
        s_last = sem("s_last")
        block = ctx.enter_context(nc.Block())

        def wait(eng, s, value):
            if not isinstance(value, int) or value > 0:
                eng.wait_ge(s, value)

        def rounds_to_last(eng, count, body):
            body(0)
            with eng.Fori(1, count - 1) as r:
                body(r)
            body(count - 1)

        def rounds(eng, count, body):
            body(0)
            with eng.Fori(1, count) as r:
                body(r)

        def blk(j):
            return slice(128 * j, 128 * j + 128)

        def half(j):
            return slice(HALF * j, HALF * j + HALF)

        def is_late(q, k):
            return isinstance(q, int) and q == ROUNDS - 1 and k >= GROUP - LATE

        def is_ahead(q, k):
            return isinstance(q, int) and q == 0 and k in (1, 2)

        def factors(q, k):
            return late[:, k - (GROUP - LATE)] if is_late(q, k) else xw[:, k % 2]

        def left_parts(i):
            if i < C - 1:
                return [(i % 2, 0, i)] if i else []
            return [(i % 2, 0, 4), (2, 4, i)]

        def counts(i, c0, c1):
            first_bank = (0, 2, 6, 4)[i] if i < 4 else (2, 3, 6, 7)[i - 4] - 1
            return bank(first_bank + c0 // HALF, (c1 - 1) // HALF + 1 - c0 // HALF
                        )[:, c0 % HALF:c0 % HALF + c1 - c0]

        PSUM3 = (0, 2, 6)

        @block.sync
        def _(sp):
            sp.dma_start(w_sb[:, :], weight).then_inc(s_in, 16)
            sp.dma_start(bias_sb[:, :], bias_col).then_inc(s_in, 16)

            def load_pairs(r):
                for k in range(XPAIRS):
                    wait(sp, s_h, (r - 1) * (2 * XPAIRS) + 2 * k + 2)
                    if isinstance(r, int) and k == 0:
                        sp.dma_start(xin[:, 0, 0, :], x[0, :, :]).then_inc(s_x_first, 16)
                        sp.dma_start(xin[:, 0, 1, :], x[1, :, :]).then_inc(s_x[0], 16)
                        continue
                    sp.dma_start(xin[:, k, :, :],
                                 x[bass.ds(r * (2 * XPAIRS) + 2 * k, 2), :, :].rearrange("b t n -> t b n")
                                 ).then_inc(s_x[k], 16)

            rounds(sp, PAIRS // XPAIRS, load_pairs)
            for i in range(C):
                if i >= GSLOTS:
                    sp.wait_ge(s_above, i - GSLOTS + 1)
                sp.dma_start(gin[:, i % GSLOTS, :, :].rearrange("p n k -> p (n k)"), gum[i, :, :]
                             ).then_inc(s_g[i % GSLOTS], 16)
            sp.wait_ge(s_above2, C - GSLOTS)

            def load_pair(k, pair):
                sp.dma_start(x2[:, k % 2, :, :], x[bass.ds(pair * 2, 2), :, :].rearrange("b t n -> t b n")
                             ).then_inc(s_x2[k % 2], 16)

            load_pair(0, 0)
            load_pair(1, 1)
            sp.wait_ge(s_left, C)
            sp.dma_start(x_early, x[4:6, :, :].rearrange("b t n -> t b n")).then_inc(s_x_early, 16)

            def stores(q):
                for k in range(GROUP):
                    pair = q * GROUP + k
                    for b in (1, 0):
                        if b == 0 and isinstance(q, int) and q == ROUNDS - 1 and k == GROUP - 1:
                            for f, step in enumerate((4, 6)):
                                sp.wait_ge(s_fold, pair * FOLD + step)
                                sp.dma_start(out[pair * 2, :, half(f)], x2[:, k % 2, 0, half(f)]
                                             ).then_inc(s_last if f else s_st[k % 2], 16)
                            continue
                        sp.wait_ge(s_fold, pair * FOLD + (FOLD - b))
                        sp.dma_start(out[bass.ds(pair * 2 + b, 1), :, :].rearrange("a t n -> t (a n)"),
                                     x2[:, k % 2, b, :]).then_inc(s_st[k % 2], 16)
                    if not (isinstance(q, int) and q == ROUNDS - 1 and k >= GROUP - 2):
                        sp.wait_ge(s_st[k % 2], q * (GROUP * 16) + (k // 2 + 1) * 32)
                        load_pair(k, pair + 2)

            rounds_to_last(sp, ROUNDS, stores)
            for slot in range(2):
                sp.wait_ge(s_st[slot], 16 * PAIRS)
            sp.wait_ge(s_last, 16)

        @block.gpsimd
        def _(pool):
            pool.memset(ones[:, :], 1.0).then_inc(s_const, 1)
            pool.memset(eps_sb[:, :], EPS / 4).then_inc(s_const, 1)
            pool.memset(hsum[:, :], 0.0).then_inc(s_const, 1)
            pool.wait_ge(s_const, 3)
            pool.affine_select(out=ident[:, :], in_=ones[:, :], compare_op=ALU.is_equal, fill=0.0, base=0,
                               pattern=[[-1, 128]], channel_multiplier=1).then_inc(s_const, 1)
            pool.wait_ge(s_const, 4)
            pool.tensor_copy(identb[:, :], ident[:, :]).then_inc(s_const, 1)
            pool.tensor_copy(identh[:, :], ident[:, :]).then_inc(s_const, 1)

            def add_even(r):
                for k in range(XPAIRS):
                    pair = r * XPAIRS + k
                    pool.wait_ge(s_h, pair * 2 + 1)
                    wait(pool, s_even, pair)
                    pool.tensor_tensor(hsum[:, :], hsum[:, :], h1[:, k % HPAIRS, 0, :], ALU.add).then_inc(s_even, 1)

            rounds(pool, PAIRS // XPAIRS, add_even)

            for i in range(GSLOTS, C):
                pool.wait_ge(s_g[i % GSLOTS], 32)
                pool.tensor_tensor(above[:, i, :], gin[:, i % GSLOTS, :, 1], gin[:, i % GSLOTS, :, 0], ALU.subtract
                                   ).then_inc(s_above2, 1)
            for i in range(1, C - 3):
                pool.wait_ge(s_edge, i + 1)
                if i > 1:
                    pool.wait_ge(s_colsum, i - 1)
                pool.tensor_tensor(wide[:, :], graph[:, 0, :] if i == 1 else wide[:, :], graph[:, i, :], ALU.add
                                   ).then_inc(s_colsum, 1)
            pool.wait_ge(s_pmax, 1)
            pool.partition_all_reduce(dmax[:, 1:2], dmax[:, 0:1], 128, RMAX).then_inc(s_gmax, 1)

            for i in range(KC):
                pool.wait_ge(s_b21r, i + 1)
                pool.tensor_tensor(b21[:, i, :], b21[:, i, :], columns, ALU.mult).then_inc(s_b21, 1)
            for i in range(KC):
                pool.wait_ge(s_b11, i + 1)
                pool.wait_ge(s_t3, i + 1)
                pool.tensor_tensor(t2[:, i, :], t3[:, i, :], b11[:, i, :], ALU.add).then_inc(s_t2, 1)
            for i in range(KC):
                pool.wait_ge(s_t2, i + 1)
                pool.wait_ge(s_b21, i + 1)
                pool.tensor_tensor(t4[:, i, :], b21[:, i, :], t2[:, i, :], ALU.subtract).then_inc(s_t4, 1)

            def add_x(q):
                for k in range(GROUP):
                    pair, slot = q * GROUP + k, k % 2
                    pool.wait_ge(s_x2[slot], q * (GROUP * 8) + (k // 2 + 1) * 16)
                    for b, f, step, u in ((0, 1, 1, fold[:, 1, :]), (1, 0, 1, fold[:, 1, :]), (1, 1, 2, fold3)):
                        pool.wait_ge(s_fold, pair * FOLD + step)
                        pool.tensor_tensor(x2[:, slot, b, half(f)], x2[:, slot, b, half(f)], u, ALU.add
                                           ).then_inc(s_y, 1)

            rounds(pool, ROUNDS, add_x)

        @block.scalar
        def _(act):
            act.wait_ge(s_const, 2)

            def std(k, pair):
                act.wait_ge(s_mv, pair + 1)
                act.activation(small[:, k % 4, 0, :], mv[:, k % 4, :, 1], ACT.Sqrt, bias=eps_sb[:, :], scale=0.25
                               ).then_inc(s_std, 1)

            def relu(k, pair):
                act.wait_ge(s_row, pair + 1)
                wait(act, s_even, pair - HPAIRS + 1)
                wait(act, s_odd, pair - HPAIRS + 1)
                for b in range(2):
                    n = pair * 2 + b
                    act.activation(h1[:, k % HPAIRS, b, :], xin[:, k % XPAIRS, b, :], ACT.Relu,
                                   bias=shift[:, bass.ds(n, 1)], scale=rstd[:, bass.ds(n, 1)]).then_inc(s_h, 1)

            def first(r):
                for k in range(XPAIRS):
                    pair = r * XPAIRS + k
                    std(k, pair)
                    if k >= 2 or not isinstance(r, int):
                        relu((k - 2) % XPAIRS, pair - 2)
                    for b in range(2):
                        if k % GROUP == 1 + b and (k > GROUP or not isinstance(r, int)):
                            keep(r * 2 + (k - GROUP - 1) // GROUP, b)

            def keep(g, b):
                n = g * 2 + b
                act.wait_ge(s_hw, n + 1)
                act.activation(kept[:, bass.ds(n, 1), :], bank(2 + 2 * b, 2).rearrange("p (a n) -> p a n", a=1),
                               ACT.Copy).then_inc(s_kept, 1)

            rounds(act, PAIRS // XPAIRS, first)
            relu(XPAIRS - 2, PAIRS - 2)
            relu(XPAIRS - 1, PAIRS - 1)
            keep(ROUNDS - 1, 0)
            keep(ROUNDS - 1, 1)

            act.wait_ge(s_sum, 1)
            act.activation(wide[:, :], hsum[:, :], ACT.Square, scale=1.0 / B).then_inc(s_sq, 1)

            def keep_late(n, first_bank):
                act.wait_ge(s_late_hw, n + 1)
                act.activation(late[:, n // 2, n % 2, :, :].rearrange("p c o -> p (c o)"), bank(first_bank, 2), ACT.Copy
                               ).then_inc(s_late, 1)

            keep_late(0, 6)
            act.wait_ge(s_guard, 1)
            act.activation(node[:, 1, :], node[:, 0, :], ACT.Sqrt).then_inc(s_root, 1)
            keep_late(1, 0)
            keep_late(2, 6)
            keep_late(3, 6)

            def h_of_pair(source, pair):
                for b in range(2):
                    n = pair * 2 + b
                    act.activation(h2[:, b, :], source[:, b, :], ACT.Relu,
                                   bias=shift[:, bass.ds(n, 1)], scale=rstd[:, bass.ds(n, 1)]).then_inc(s_h2, 1)

            act.wait_ge(s_x2[1], 16)
            h_of_pair(x2[:, 1], 1)

            def count(i):
                act.wait_ge(s_nm, i + 1)
                if i:
                    act.wait_ge(s_cnt, i)
                act.activation(hsum[:, :], nmask[:, i, :], ACT.Copy, accum_out=node[:, 6, i:i + 1]
                               ).then_inc(s_cnt, 1)

            for i in range(C - 1):
                count(i)

            for i in range(C):
                act.wait_ge(s_com, i + 1)
                if i < C - 1:
                    act.activation(right[:, RIGHT[i]:RIGHT[i + 1]], counts(i, 128 * (i + 1), N), ACT.Copy
                                   ).then_inc(s_right, 1)
                if i >= 2:
                    act.wait_ge(s_edge, i - 1)
                act.activation(squares[:, i % 2, 128 * i:N], counts(i, 128 * i, N), ACT.Square).then_inc(s_csq, 1)
                for part, (bank_, j0, j1) in enumerate(left_parts(i)):
                    act.wait_ge(s_left, i + part)
                    act.activation(squares[:, i % 2, 128 * j0:128 * j1],
                                   ps[:, bank_, :].bitcast(FP16)[:, 128 * j0:128 * j1], ACT.Square).then_inc(s_lsq, 1)
            count(C - 1)

            def take(k, q):
                for b in range(2):
                    to = xw[:, k % 2, b, :, :].rearrange("p c o -> p (c o)")
                    if k == 0:
                        act.activation(to.rearrange("p (a n) -> p a n", a=1), kept[:, bass.ds(q * 2 + b, 1), :],
                                       ACT.Copy).then_inc(s_xw, 1)
                    else:
                        act.wait_ge(s_hw2, q * (2 * GROUP - 2) + 2 * k + b - 1)
                        act.activation(to, bank(4 + 2 * b, 2), ACT.Copy).then_inc(s_xw, 1)

            act.wait_ge(s_above2, C - GSLOTS)
            take(0, 0)
            act.wait_ge(s_edge, C + 1)
            take(1, 0)
            act.wait_ge(s_x_early, 16)
            act.wait_ge(s_hw2, 2)
            h_of_pair(x_early, 2)
            act.wait_ge(s_guard, 2)
            act.activation(node[:, 1, :], node[:, 0, :], ACT.Sqrt).then_inc(s_root, 1)
            act.wait_ge(s_rep, 3)
            act.activation(columns, ps[:, 2, :], ACT.Copy).then_inc(s_repc, 1)
            act.wait_ge(s_rows, 1)
            for i in range(KC, C):
                act.activation(graph[:, i, 0:HALF], graph[:, i, 0:HALF], ACT.Copy, scale=node[:, 9, i:i + 1]
                               ).then_inc(s_b21r, 1)

            def second(q):
                for k in range(GROUP):
                    pair = q * GROUP + k
                    act.wait_ge(s_prod, pair * PROD + 1)
                    wait(act, s_fold, pair * FOLD - FOLD + 1)
                    act.activation(fold[:, 0, :], ps[:, 0, :], ACT.Identity, bias=bias_sb[:, :]).then_inc(s_p1, 1)
                    if is_late(q, k + 1) or (is_ahead(q, k + 1) and k == 0):
                        continue
                    if k + 1 < GROUP and not is_ahead(q, k + 1):
                        act.wait_ge(s_x2[(k + 1) % 2], q * (GROUP * 8) + ((k + 1) // 2 + 1) * 16)
                        wait(act, s_hw2, q * (2 * GROUP - 2) + 2 * k)
                        h_of_pair(x2[:, (k + 1) % 2], pair + 1)
                    if k + 1 < GROUP:
                        take(k + 1, q)
                    elif not (isinstance(q, int) and q == ROUNDS - 1):
                        take(0, q + 1)

            rounds_to_last(act, ROUNDS, second)

        @block.vector
        def _(dve):
            dve.wait_ge(s_const, 5)
            dve.wait_ge(s_in, 32)

            def rows(k):
                return (*(small[:, k % 4, c, :] for c in range(4)), mv[:, k % 4, :, 0], mv[:, k % 4, :, 1])

            def aggregate(k):
                for b in range(2):
                    last = dve.bn_aggr(mv[:, k % 4, b, :], stats[:, k % 2, b, :])
                last.then_inc(s_mv, 1)

            def invert(k, pair):
                half_std, _, _, inv, *_ = rows(k)
                dve.wait_ge(s_std, pair + 1)
                dve.reciprocal(inv, half_std).then_inc(s_inv, 1)

            def quotient(k, pair):
                _, quot, _, inv, _, var = rows(k)
                dve.wait_ge(s_inv, pair + 1)
                dve.scalar_tensor_tensor(out=quot, in0=var, scalar=EPS, in1=inv, op0=ALU.add, op1=ALU.mult
                                         ).then_inc(s_quot, 1)

            def newton(k, pair):
                half_std, quot, std_, *_ = rows(k)
                dve.wait_ge(s_quot, pair + 1)
                dve.scalar_tensor_tensor(out=std_, in0=quot, scalar=0.25, in1=half_std, op0=ALU.mult, op1=ALU.add
                                         ).then_inc(s_newton, 1)

            def set_rstd(k, pair):
                dve.wait_ge(s_newton, pair + 1)
                dve.reciprocal(rstd[:, bass.ds(pair * 2, 2)], rows(k)[2]).then_inc(s_rstd, 1)

            def set_shift(k, pair):
                mean = rows(k)[4]
                here = bass.ds(pair * 2, 2)
                dve.wait_ge(s_rstd, pair + 1)
                dve.scalar_tensor_tensor(out=shift[:, here], in0=mean, scalar=-1.0, in1=rstd[:, here],
                                         op0=ALU.mult, op1=ALU.mult).then_inc(s_row, 1)

            def first(r):
                for k in range(XPAIRS):
                    pair = r * XPAIRS + k
                    one_before = k >= 1 or not isinstance(r, int)
                    two_before = k >= 2 or not isinstance(r, int)

                    def long_step(c):
                        b, f = divmod(c, 2)
                        return dve.bn_stats(stats[:, k % 2, b, 6 * f:6 * f + 6], xin[:, k, b, half(f)])

                    if isinstance(r, int) and k == 0:
                        dve.wait_ge(s_x_first, 16)
                    else:
                        dve.wait_ge(s_x[k], (r + 1) * 16)
                    long_step(0)
                    if one_before:
                        dve.wait_ge(s_bn, pair)
                        if two_before:
                            newton(k - 2, pair - 2)
                        aggregate(k - 1)
                    long_step(1)
                    if two_before:
                        set_rstd(k - 2, pair - 2)
                    if isinstance(r, int) and k == 0:
                        dve.wait_ge(s_x[0], 16)
                    long_step(2)
                    if one_before:
                        invert(k - 1, pair - 1)
                    long_step(3).then_inc(s_bn, 1)
                    if one_before:
                        quotient(k - 1, pair - 1)
                    if two_before:
                        set_shift(k - 2, pair - 2)

            rounds(dve, PAIRS // XPAIRS, first)
            dve.wait_ge(s_bn, PAIRS)
            aggregate(PAIRS - 1)
            one, two = PAIRS - 1, PAIRS - 2
            newton(two, two)
            invert(one, one)
            set_rstd(two, two)
            quotient(one, one)
            set_shift(two, two)
            newton(one, one)
            set_rstd(one, one)
            set_shift(one, one)

            chain = [0]

            def step(ins):
                chain[0] += 1
                ins.then_inc(s_dve, 1)
                dve.wait_ge(s_dve, chain[0])

            def inverse_root(n, scale):
                dve.wait_ge(s_root, n)
                step(dve.reciprocal(node[:, 2, :], node[:, 1, :]))
                step(dve.tensor_tensor(node[:, 3, :], node[:, 2, :], node[:, 2, :], ALU.mult))
                step(dve.tensor_tensor(node[:, 4, :], node[:, 3, :], node[:, 0, :], ALU.mult))
                step(dve.tensor_scalar(node[:, 3, :], node[:, 4, :], -0.5, 1.5, ALU.mult, ALU.add))
                step(dve.scalar_tensor_tensor(out=node[:, 5, :], in0=node[:, 3, :], scalar=scale, in1=node[:, 2, :],
                                              op0=ALU.mult, op1=ALU.mult))

            def diagonal():
                for j in range(C):
                    dve.tensor_scalar(wide[:, blk(j)], ident[:, :], node[:, 5, j:j + 1], None, ALU.mult
                                      ).then_inc(s_diag, 1)

            def threshold(i):
                dve.wait_ge(s_h, 2 * PAIRS - XPAIRS)
                dve.wait_ge(s_g[i], 16)
                dve.tensor_tensor(above[:, i, :], gin[:, i, :, 1], gin[:, i, :, 0], ALU.subtract
                                  ).then_inc(s_above, 1)

            for i in range(GSLOTS - 1):
                threshold(i)
            dve.wait_ge(s_odd, PAIRS)
            dve.wait_ge(s_even, PAIRS)
            dve.tensor_tensor(hsum[:, :], bank(0, 2), hsum[:, :], ALU.add).then_inc(s_sum, 1)
            threshold(GSLOTS - 1)
            dve.wait_ge(s_col, 1)
            dve.tensor_scalar(node[:, 0, :], ps[:, 2, 0:C], 1e-24, None, ALU.max).then_inc(s_guard, 1)
            inverse_root(1, 1.0 / B)
            diagonal()
            for f in range(2):
                dve.wait_ge(s_rep, f + 1)
                dve.tensor_tensor(hsum[:, half(f)], ps[:, 4 + f, :], hsum[:, half(f)], ALU.mult).then_inc(s_unit, 1)

            for i in range(C):
                if i < GSLOTS:
                    dve.wait_ge(s_above, i + 1)
                else:
                    dve.wait_ge(s_above2, i - GSLOTS + 1)
                dve.wait_ge(s_dot, i + 1)
                dve.tensor_tensor(adj[:, i, :], bank(PSUM3[i % 3], 2), above[:, i, :], ALU.is_gt).then_inc(s_adj, 1)
            dve.wait_ge(s_late_hw, 2 * LATE)
            for i in range(C):
                dve.wait_ge(s_tr, i + 1)
                dve.tensor_tensor(nmask[:, i, :], ps[:, 4 + i % 2, :].bitcast(BF16), adj[:, i, :], ALU.max
                                  ).then_inc(s_sym, 1)
                dve.wait_ge(s_sym, i + 1)
                dve.tensor_tensor(nmask[:, i, blk(i)], nmask[:, i, blk(i)], identb[:, :], ALU.max).then_inc(s_nm, 1)

            def combine(q, k, pair):
                a = factors(q, k)
                a11, a12, a21, a22 = a[:, 0, 0:KC, :], a[:, 0, KC:C, :], a[:, 1, 0:KC, :], a[:, 1, KC:C, :]
                s1, s2, s3, s4 = (sums[:, k % 2, c, :, :] for c in range(4))
                if is_late(q, k):
                    dve.wait_ge(s_late, 2 * LATE)
                else:
                    dve.wait_ge(s_xw, pair * 2 + 2)
                dve.tensor_tensor(s1, a21, a22, ALU.add).then_inc(s_comb, 1)
                dve.tensor_tensor(s3, a11, a21, ALU.subtract).then_inc(s_comb, 1)
                dve.wait_ge(s_comb, pair * 4 + 1)
                dve.tensor_tensor(s2, s1, a11, ALU.subtract).then_inc(s_comb, 1)
                dve.wait_ge(s_comb, pair * 4 + 3)
                dve.tensor_tensor(s4, a12, s2, ALU.subtract).then_inc(s_comb, 1)

            for i in range(C):
                for f in range(1 if i < C - 1 else 2):
                    cols = slice(0, N) if i < C - 1 else half(f)
                    if i:
                        dve.wait_ge(s_lsq, i + f)
                    if i < C - 1 or f:
                        dve.wait_ge(s_csq, i + 1)
                        diag = squares[:, i % 2, blk(i)]
                        dve.scalar_tensor_tensor(out=diag, in0=diag, scalar=1.0, in1=diag, op0=ALU.is_gt,
                                                 op1=ALU.mult).then_inc(s_mask, 1)
                        dve.wait_ge(s_mask, i + 1)
                    dve.tensor_tensor(graph[:, i, cols], squares[:, i % 2, cols], adj[:, i, cols], ALU.mult
                                      ).then_inc(s_edge, 1)

            for f in range(2):
                dve.wait_ge(s_edge, C + f)
                dve.tensor_tensor(squares[:, 0, half(f)], graph[:, C - 2, half(f)], graph[:, C - 1, half(f)], ALU.add
                                  ).then_inc(s_two, 1)
            combine(0, 0, 0)
            dve.wait_ge(s_cnt, C)
            dve.reduce_max(dmax[:, 0:1], node[:, 6, :], AX_X).then_inc(s_pmax, 1)

            dve.wait_ge(s_gmax, 1)
            step(dve.reciprocal(dmax[:, 2:3], dmax[:, 1:2]))
            dve.wait_ge(s_col, 2)
            step(dve.tensor_scalar(node[:, 7, :], ps[:, 0, 0:C], dmax[:, 2:3], None, ALU.mult))
            dve.tensor_scalar(node[:, 0, :], node[:, 7, :], 1e-6, None, ALU.max).then_inc(s_guard, 1)
            step(dve.tensor_scalar(node[:, 8, :], node[:, 7, :], 0.0, None, ALU.is_gt))
            inverse_root(2, 1.0)
            step(dve.tensor_tensor(node[:, 5, :], node[:, 5, :], node[:, 8, :], ALU.mult))
            dve.tensor_scalar(node[:, 9, :], node[:, 5, :], dmax[:, 2:3], None, ALU.mult).then_inc(s_rows, 1)
            diagonal()
            dve.wait_ge(s_rows, 1)
            def scaled(i, f, factors):
                return dve.scalar_tensor_tensor(out=graph[:, i, half(f)], in0=graph[:, i, half(f)],
                                                scalar=node[:, 9, i:i + 1], in1=factors, op0=ALU.mult, op1=ALU.mult)

            dve.wait_ge(s_repc, 1)
            for i in range(KC):
                scaled(i, 0, columns).then_inc(s_b11, 1)
            dve.wait_ge(s_rep, 4)
            for i in range(KC):
                scaled(i, 1, ps[:, 3, :]).then_inc(s_b2, 1)
                scaled(KC + i, 1, ps[:, 3, :]).then_inc(s_b2, 1)
                dve.wait_ge(s_b2, 2 * i + 2)
                dve.tensor_tensor(t3[:, i, :], b22[:, i, :], b12[:, i, :], ALU.subtract).then_inc(s_t3, 1)
            for i in range(KC):
                dve.wait_ge(s_t3, i + 1)
                dve.wait_ge(s_b11, i + 1)
                dve.tensor_tensor(t1[:, i, :], b12[:, i, :], b11[:, i, :], ALU.subtract).then_inc(s_t1, 1)

            def second(q):
                for k in range(GROUP):
                    pair, slot = q * GROUP + k, k % 2
                    bank_a, bank_b, bank_c, bank_d = (ps[:, c, :] for c in range(4))
                    u2 = fold[:, 1, :]
                    late = 1 if isinstance(q, int) and q == k == 0 else 0
                    dve.wait_ge(s_p1, pair + 1)
                    dve.wait_ge(s_prod, pair * PROD + 3 + late)
                    wait(dve, s_y, pair * 3 - 1)
                    dve.tensor_tensor(u2, bank_b, fold[:, 0, :], ALU.add).then_inc(s_fold, 1)
                    dve.wait_ge(s_fold, pair * FOLD + 1)
                    wait(dve, s_y, pair * 3)
                    dve.tensor_tensor(fold3, bank_c, u2, ALU.add).then_inc(s_fold, 1)

                    def result(b, f, product, bank_):
                        dve.wait_ge(s_prod, pair * PROD + product)
                        dve.tensor_tensor(x2[:, slot, b, half(f)], bank_, x2[:, slot, b, half(f)], ALU.add
                                          ).then_inc(s_fold, 1)

                    dve.wait_ge(s_y, pair * 3 + 3)
                    result(1, 1, 4 + late, bank_d)
                    dve.wait_ge(s_prod, pair * PROD + 5)
                    dve.scalar_tensor_tensor(out=x2[:, slot, 0, half(0)], in0=bank_a, scalar=bias_sb[:, :],
                                             in1=x2[:, slot, 0, half(0)], op0=ALU.add, op1=ALU.add
                                             ).then_inc(s_fold, 1)
                    if k + 1 < GROUP:
                        combine(q, k + 1, pair + 1)
                    elif not (isinstance(q, int) and q == ROUNDS - 1):
                        combine(q + 1, 0, pair + 1)
                    result(1, 0, 6, bank_c)
                    result(0, 1, 7, bank_d)

            rounds_to_last(dve, ROUNDS, second)

        @block.tensor
        def _(pe):
            pe.wait_ge(s_const, 6)
            pe.wait_ge(s_in, 32)

            def times_weight(h, first_bank):
                for c in range(C):
                    last = pe.matmul(ps[:, first_bank + c // 4, blk(c % 4)], h[:, blk(c)], w_sb[:, :],
                                     start=True, stop=True)
                return last

            def first(r):
                for k in range(XPAIRS):
                    pair = r * XPAIRS + k
                    if k % 4 == 0:
                        for b in range(2):
                            n = r * 4 + k // 4 * 2 + b
                            pe.wait_ge(s_h, pair * 2 + b + 1)
                            wait(pe, s_kept, n - 1)
                            times_weight(h1[:, k % HPAIRS, b, :], 2 + 2 * b).then_inc(s_hw, 1)
                    pe.wait_ge(s_h, pair * 2 + 2)
                    for f in range(2):
                        last = pe.matmul(ps[:, f, :], ident[:, :], h1[:, k % HPAIRS, 1, half(f)],
                                         start=isinstance(r, int) and k == 0, stop=True, skip_group_check=True)
                    last.then_inc(s_odd, 1)

            rounds(pe, PAIRS // XPAIRS, first)

            def column_sums(b):
                for j in range(C):
                    last = pe.matmul(ps[:, b, j:j + 1], wide[:, blk(j)], ones[:, 0:1], start=True, stop=True)
                last.then_inc(s_col, 1)

            def replicate(first_bank, before):
                for j in range(C):
                    pe.wait_ge(s_diag, before + j + 1)
                    last = pe.matmul(ps[:, first_bank + j // 4, blk(j % 4)], ones[:, :], wide[:, blk(j)],
                                     start=True, stop=True)
                    if j % 4 == 3:
                        last.then_inc(s_rep, 1)

            pe.wait_ge(s_kept, KEPT)

            def late_times_weight(n, first_bank):
                pair = PAIRS - LATE + n // 2
                times_weight(h1[:, pair % HPAIRS, n % 2, :], first_bank).then_inc(s_late_hw, 1)

            late_times_weight(0, 6)
            pe.wait_ge(s_sq, 1)
            column_sums(2)
            late_times_weight(1, 0)
            replicate(4, 0)
            pe.wait_ge(s_late, 1)
            late_times_weight(2, 6)
            pe.wait_ge(s_unit, 2)
            pe.wait_ge(s_late, 2)
            for i in range(C):
                if i == 2:
                    pe.wait_ge(s_late, 3)
                if i >= 3:
                    pe.wait_ge(s_adj, i - 2)
                for f in range(2):
                    last = pe.matmul(ps[:, PSUM3[i % 3] + f, :], hsum[:, blk(i)], hsum[:, half(f)],
                                     start=True, stop=True)
                last.then_inc(s_dot, 1)
            pe.wait_ge(s_adj, C - 2)
            late_times_weight(3, 6)
            pe.wait_ge(s_adj, C)

            def transposes(i):
                if i >= 2:
                    pe.wait_ge(s_sym, i - 1)
                for j in range(C):
                    last = pe.transpose(ps[:, 4 + i % 2, :].bitcast(BF16)[:, blk(j)], adj[:, j, blk(i)], identb[:, :])
                last.then_inc(s_tr, 1)

            def common(i, k):
                for f in range(2):
                    cols = slice(max(128 * i, HALF * f), HALF * (f + 1))
                    if cols.start < cols.stop:
                        last = pe.matmul(counts(i, cols.start, cols.stop), nmask[:, k, blk(i)], nmask[:, k, cols],
                                         start=k == 0, stop=k == C - 1)
                if k == C - 1:
                    last.then_inc(s_com, 1)

            def left(i):
                for part, (bank_, j0, j1) in enumerate(left_parts(i)):
                    if part:
                        pe.wait_ge(s_csq, 5)
                    elif i >= 3:
                        pe.wait_ge(s_lsq, i - 2)
                    else:
                        pe.wait_ge(s_csq, 1)
                    pe.wait_ge(s_right, j1)
                    for j in range(j0, j1):
                        at = RIGHT[j] + 128 * (i - j - 1)
                        last = pe.transpose(ps[:, bank_, :].bitcast(FP16)[:, blk(j)], right[:, at:at + 128],
                                            identh[:, :])
                    last.then_inc(s_left, 1)

            transposes(0)
            transposes(1)
            for k in range(C):
                pe.wait_ge(s_nm, k + 1)
                for i in range(3):
                    if k == 0 and i == 2:
                        pe.wait_ge(s_late, 4)
                    common(i, k)
                if k + 2 < C:
                    transposes(k + 2)

            def ahead(n):
                b = n % 2
                pe.wait_ge(s_h2, n + 1)
                if n >= 2:
                    pe.wait_ge(s_xw, 4)
                times_weight(h2[:, b, :], 4 + 2 * b).then_inc(s_hw2, 1)

            for i in range(3, C):
                if i == 3:
                    pe.wait_ge(s_sym, C)
                else:
                    pe.wait_ge(s_csq, 2 if i < 6 else 3)
                for k in range(C):
                    common(i, k)
                if i == 3:
                    left(1)
                    left(2)
                left(i)
                if i == 6:
                    pe.wait_ge(s_csq, 4)
                    ahead(0)

            pe.wait_ge(s_lsq, C - 2)
            for part, source in enumerate((graph[:, C - 3, :], wide[:, :], squares[:, 0, :])):
                if part == 0:
                    pe.wait_ge(s_edge, C - 2)
                if part == 1:
                    pe.wait_ge(s_csq, C)
                    ahead(1)
                    pe.wait_ge(s_colsum, C - 4)
                for j in range(C):
                    if part == 2:
                        pe.wait_ge(s_two, j // KC + 1)
                    last = pe.matmul(ps[:, 0, j:j + 1], source[:, blk(j)], ones[:, 0:1], start=part == j == 0,
                                     stop=True, skip_group_check=True)
            last.then_inc(s_col, 1)
            ahead(2)
            ahead(3)
            pe.wait_ge(s_lsq, C)
            replicate(2, C)

            def product(a, b_, bank_, onto, made=None):
                for c in range(KC):
                    if made:
                        pe.wait_ge(made, c + 1)
                    last = pe.matmul(ps[:, bank_, :], a[:, c, :], b_[:, c, :], start=not onto and c == 0,
                                     stop=c == KC - 1, skip_group_check=True)
                last.then_inc(s_prod, 1)

            def second(q):
                for k in range(GROUP):
                    pair, slot = q * GROUP + k, k % 2
                    start = isinstance(q, int) and q == k == 0
                    a = factors(q, k)
                    a11, a12, a22 = (a[:, b, c:c + KC, :] for b, c in ((0, 0), (0, KC), (1, KC)))
                    s1, s2, s3, s4 = (sums[:, slot, c, :, :] for c in range(4))
                    if is_late(q, k):
                        pe.wait_ge(s_late, 2 * LATE)
                    else:
                        pe.wait_ge(s_xw, pair * 2 + 2)
                    wait(pe, s_fold, pair * FOLD - 2)
                    product(a11, b11, 0, False, start and s_b11)
                    if start:
                        pe.wait_ge(s_p1, 1)
                        product(a12, b21, 0, True, s_b21)
                    pe.wait_ge(s_comb, pair * 4 + 4)
                    wait(pe, s_fold, pair * FOLD - 1)
                    if start:
                        pe.wait_ge(s_repc, 1)
                    product(s3, t3, 2, False, start and s_t3)
                    product(s2, t2, 1, False, start and s_t2)
                    wait(pe, s_fold, pair * FOLD)
                    if start:
                        pe.wait_ge(s_b2, 2 * KC)
                    product(s1, t1, 3, False, start and s_t1)
                    if not start:
                        pe.wait_ge(s_p1, pair + 1)
                        product(a12, b21, 0, True)
                    if k + 1 < GROUP and not is_ahead(q, k + 1) and not is_late(q, k + 1):
                        for b in range(2):
                            pe.wait_ge(s_h2, q * (2 * GROUP - 2) + 2 * k + b + 1)
                            times_weight(h2[:, b, :], 4 + 2 * b).then_inc(s_hw2, 1)
                    pe.wait_ge(s_fold, pair * FOLD + 2)
                    product(a22, t4, 2, True, start and s_t4)
                    pe.wait_ge(s_fold, pair * FOLD + 3)
                    product(s4, b22, 3, True)

            rounds_to_last(pe, ROUNDS, second)


_INS = ["x", "adj", "L0_gnn_bias", "L0_gnn_gumbel"]


def kernel(**inputs):
    import numpy as _np
    import concourse.bacc as _bacc
    from concourse import mybir as _mybir
    from concourse.bass_utils import run_bass_kernel_spmd as _run

    nc = _bacc.Bacc("TRN2", target_bir_lowering=False, num_devices=1)
    arrays, args = {}, []
    for name in _INS:
        a = _np.ascontiguousarray(inputs[name])
        arrays[f"in_{name}"] = a
        args.append(nc.dram_tensor(f"in_{name}", a.shape, _mybir.dt.from_np(a.dtype), kind="ExternalInput").ap())
    shape = arrays["in_x"].shape
    args.append(nc.dram_tensor("out_0", shape, FP32, kind="ExternalOutput").ap())
    gnn_kernel(nc, *args)
    r = _run(nc, [arrays], core_ids=[0])
    return r.results[0]["out_0"]
```
